# Optimizing a Trainium2 kernel written in Bass

```python
import numpy as np
import jax
import jax.numpy as jnp

def _softmax(x, axis=-1):
    return jax.nn.softmax(x, axis=axis)

def _gelu(x):
    return jax.nn.gelu(x, approximate=True)

def _silu(x):
    return jax.nn.silu(x)

def _sigmoid(x):
    return jax.nn.sigmoid(x)

def _layernorm(x, axis=-1, eps=1e-05):
    m = jnp.mean(x, axis=axis, keepdims=True)
    v = jnp.var(x, axis=axis, keepdims=True)
    return (x - m) / jnp.sqrt(v + eps)

def _scatter_add(tgt, idx, src, axis=0):
    return tgt.at[idx].add(src)

def _segment_sum(src, seg, n):
    return jax.ops.segment_sum(src, seg, n)
kernel_name = 'mk_adj_ffn_d1_adj_r2_8359d7'

def setup_inputs(seed: int=0):
    np.random.seed(seed)
    _w = jnp.asarray

    def _rec_inputs():
        import jax
        import jax.numpy as jnp
        _gk = jax.random.key(seed)
        x = -0.0005207 + 1.001 * jax.random.normal(jax.random.fold_in(_gk, 1), (3327, 128), jnp.float32)
        _a = jax.random.bernoulli(jax.random.fold_in(_gk, 2), 0.00961827, (3327, 3327))
        adj = _a.astype(jnp.int32)
        return (x, adj)
    x, adj = _rec_inputs()

    def _L0_gnn_setup():
        import jax, jax.numpy as jnp
        import numpy as np
        ALPHA = 0.2
        NEG_FILL = -9000000000000000.0
        key = jax.random.key(seed)
        k_h, k_adj, k_W, k_a = jax.random.split(key, 4)
        N, D_IN, D_OUT = (4096, 128, 128)
        h = jax.random.normal(k_h, (N, D_IN), dtype=jnp.float32)
        adj = jax.random.randint(k_adj, (N, N), 0, 2, dtype=jnp.int32)
        W = jax.random.normal(k_W, (D_IN, D_OUT), dtype=jnp.float32) * (1.414 * np.sqrt(2.0 / (D_IN + D_OUT)))
        a = jax.random.normal(k_a, (2 * D_OUT, 1), dtype=jnp.float32) * (1.414 * np.sqrt(2.0 / (2 * D_OUT + 1)))
        return {'h': h, 'adj': adj, 'W': W, 'a': a}
    _L0_gnn_all = _L0_gnn_setup()
    _L0_gnn_in = {k: v for k, v in _L0_gnn_all.items() if k in ('W', 'a')}
    del _L0_gnn_all

    def _L0_ffn_setup():
        import jax, jax.numpy as jnp
        import numpy as np
        DIM = 128
        HEADS = 8
        NUM_KEYS = 128
        NUM_KV = NUM_KEYS ** 2
        PK_TOPK = 16
        FINAL_TOPK = 16
        DIM_KEY = DIM // 2
        P = 2

        def _pk(x, Wq_pk, pk_keys):
            b, n, _ = x.shape
            q = (x @ Wq_pk).reshape(b, n, P, HEADS, DIM_KEY).transpose(2, 0, 1, 3, 4)
            sim = jnp.einsum('pbnhd,pkhd->pbnhk', q, pk_keys)
            scores, idx = jax.lax.top_k(sim, PK_TOPK)
            idx0 = idx[0]
            idx1 = idx[1] * NUM_KEYS
            index = (idx0[..., :, None] + idx1[..., None, :]).reshape(b, n, HEADS, PK_TOPK * PK_TOPK)
            score = (scores[0][..., :, None] + scores[1][..., None, :]).reshape(b, n, HEADS, PK_TOPK * PK_TOPK)
            final_scores, pk_idx = jax.lax.top_k(score, FINAL_TOPK)
            final_indices = jnp.take_along_axis(index, pk_idx, axis=-1)
            final_scores = jax.nn.softmax(final_scores, axis=-1)
            return (final_scores, final_indices)
        key = jax.random.key(seed)
        ks = jax.random.split(key, 7)
        b, n = (2, 512)
        std = 0.02
        x = jax.random.normal(ks[0], (b, n, DIM), dtype=jnp.float32)
        Wq_pk = jax.random.normal(ks[1], (DIM, P * HEADS * DIM_KEY), dtype=jnp.float32) * std
        pk_keys = jax.random.normal(ks[2], (P, NUM_KEYS, HEADS, DIM_KEY), dtype=jnp.float32) * std
        Wq = jax.random.normal(ks[3], (DIM, HEADS * DIM), dtype=jnp.float32) * std
        keys_table = jax.random.normal(ks[4], (NUM_KV * HEADS, DIM), dtype=jnp.float32) * std
        values_table = jax.random.normal(ks[5], (NUM_KV * HEADS, DIM), dtype=jnp.float32) * std
        Wo = jax.random.normal(ks[6], (DIM * HEADS, DIM), dtype=jnp.float32) * std
        return {'x': x, 'Wq_pk': Wq_pk, 'pk_keys': pk_keys, 'Wq': Wq, 'keys_table': keys_table, 'values_table': values_table, 'Wo': Wo}
    _L0_ffn_all = _L0_ffn_setup()
    _L0_ffn_in = {k: v for k, v in _L0_ffn_all.items() if k in ('Wq_pk', 'pk_keys', 'Wq', 'keys_table', 'values_table', 'Wo')}
    del _L0_ffn_all
    return {'x': x, 'adj': adj, 'L0_gnn_W': _L0_gnn_in['W'], 'L0_gnn_a': _L0_gnn_in['a'], 'L0_ffn_Wq_pk': _L0_ffn_in['Wq_pk'], 'L0_ffn_pk_keys': _L0_ffn_in['pk_keys'], 'L0_ffn_Wq': _L0_ffn_in['Wq'], 'L0_ffn_keys_table': _L0_ffn_in['keys_table'], 'L0_ffn_values_table': _L0_ffn_in['values_table'], 'L0_ffn_Wo': _L0_ffn_in['Wo']}

def reference(x, adj, L0_gnn_W, L0_gnn_a, L0_ffn_Wq_pk, L0_ffn_pk_keys, L0_ffn_Wq, L0_ffn_keys_table, L0_ffn_values_table, L0_ffn_Wo):
    import jax
    import jax.numpy as jnp

    def _L0_gnn_ref(h, adj, W, a):
        import jax, jax.numpy as jnp
        import numpy as np
        ALPHA = 0.2
        NEG_FILL = -9000000000000000.0
        d_out = W.shape[1]
        Wh = h @ W
        Wh1 = Wh @ a[:d_out]
        Wh2 = Wh @ a[d_out:]
        e = Wh1 + Wh2.T
        e = jnp.where(e > 0, e, ALPHA * e)
        scores = jnp.where(adj > 0, e, NEG_FILL)
        attention = jax.nn.softmax(scores, axis=1)
        h_prime = attention @ Wh
        return jax.nn.elu(h_prime)

    def _L0_ffn_ref(x, Wq_pk, pk_keys, Wq, keys_table, values_table, Wo):
        import jax, jax.numpy as jnp
        import numpy as np
        DIM = 128
        HEADS = 8
        NUM_KEYS = 128
        NUM_KV = NUM_KEYS ** 2
        PK_TOPK = 16
        FINAL_TOPK = 16
        DIM_KEY = DIM // 2
        P = 2

        def _pk(x, Wq_pk, pk_keys):
            b, n, _ = x.shape
            q = (x @ Wq_pk).reshape(b, n, P, HEADS, DIM_KEY).transpose(2, 0, 1, 3, 4)
            sim = jnp.einsum('pbnhd,pkhd->pbnhk', q, pk_keys)
            scores, idx = jax.lax.top_k(sim, PK_TOPK)
            idx0 = idx[0]
            idx1 = idx[1] * NUM_KEYS
            index = (idx0[..., :, None] + idx1[..., None, :]).reshape(b, n, HEADS, PK_TOPK * PK_TOPK)
            score = (scores[0][..., :, None] + scores[1][..., None, :]).reshape(b, n, HEADS, PK_TOPK * PK_TOPK)
            final_scores, pk_idx = jax.lax.top_k(score, FINAL_TOPK)
            final_indices = jnp.take_along_axis(index, pk_idx, axis=-1)
            final_scores = jax.nn.softmax(final_scores, axis=-1)
            return (final_scores, final_indices)
        b, n, d = x.shape
        q = (x @ Wq).reshape(b, n, HEADS, DIM) * DIM ** (-0.5)
        kv_scores, indices = _pk(x, Wq_pk, pk_keys)
        offsets = jnp.arange(HEADS, dtype=indices.dtype) * NUM_KV
        ind = indices + offsets[None, None, :, None]
        k = jnp.einsum('bnhk,bnhkd->bnhd', kv_scores, keys_table[ind])
        v = jnp.einsum('bnhk,bnhkd->bnhd', kv_scores, values_table[ind])
        sim = jnp.einsum('bihd,bjhd->bhij', q, k)
        neg = -jnp.finfo(sim.dtype).max
        causal = jnp.tril(jnp.ones((n, n), dtype=bool))
        sim = jnp.where(causal, sim, neg)
        attn = jax.nn.softmax(sim, axis=-1)
        out = jnp.einsum('bhij,bjhd->bhid', attn, v)
        out = out.transpose(0, 2, 1, 3).reshape(b, n, HEADS * DIM)
        return out @ Wo
    x = x + _L0_gnn_ref(_layernorm(x, axis=-1), adj, L0_gnn_W, L0_gnn_a)
    x = x + _L0_ffn_ref(_layernorm(x, axis=-1)[None], L0_ffn_Wq_pk, L0_ffn_pk_keys, L0_ffn_Wq, L0_ffn_keys_table, L0_ffn_values_table, L0_ffn_Wo)[0]
    return x

_drawn_inputs = setup_inputs


def setup_inputs(seed=0):
    import zlib

    import numpy as np

    out = dict(_drawn_inputs(seed))
    spreads = {}
    factors = {'L0_ffn_Wq_pk': 31.738,
     'L0_ffn_pk_keys': 31.665,
     'L0_ffn_Wq': 64.0,
     'L0_ffn_keys_table': 64.0,
     'L0_ffn_values_table': 28.291,
     'L0_ffn_Wo': 28.081}
    for name, (base, spread) in spreads.items():
        noise = np.random.default_rng([zlib.crc32(name.encode()), seed]).standard_normal(out[name].shape)
        drawn = base * np.exp(spread * noise) if base else spread * noise
        out[name] = jnp.asarray(drawn.astype(out[name].dtype))
    for name, factor in factors.items():
        out[name] = (out[name] * factor).astype(out[name].dtype)
    return out
```

```python
import concourse.bass as bass
from concourse import mybir
from contextlib import ExitStack


def gat_then_product_key_attention(nc, x, adj, W, WT, a, wqpkT, keysT, Wq, kv_table, Wo, out):
    f32, bf16, u32, i32 = mybir.dt.float32, mybir.dt.bfloat16, mybir.dt.uint32, mybir.dt.int32
    ALU = mybir.AluOpType
    ACT = mybir.ActivationFunctionType
    AX = mybir.AxisListType

    P = 128
    N, D = x.shape
    NT = -(-N // P)
    NP = NT * P
    REST = N - (NT - 1) * P
    PS, H, DK, NK = keysT.shape
    TOP = 16
    C = 4
    CH = C * P
    ALPHA = 0.2
    MASKED = -9000000000000000.0
    FUTURE = -1e30
    LOWEST = -3.4028234663852886e38
    EPS = 1e-5
    SCALE = float(D) ** -0.5
    KV = 2 * D
    chunks_of = [-(-(t + 1) // C) for t in range(NT)]
    chunk_at = [sum(chunks_of[:t]) for t in range(NT + 1)]
    NCH = chunk_at[NT]
    GC = -(-NT // C)
    assert D == P and NK == P and PS == 2 and NT % 2 == 0 and NCH % 2 == 0 and NT >= 4 and GC % 2 == 1
    SPLIT = (REST // 16) * 16

    ctx = ExitStack()
    with ctx:
        def sb(name, shape, dt=f32):
            return ctx.enter_context(nc.sbuf_tensor(name, shape, dt))

        def bank(name):
            return ctx.enter_context(nc.psum_tensor(name, [P, 512], f32))

        def sem(name):
            return ctx.enter_context(nc.semaphore(name))

        xs = sb("xs", [P, NT, D])
        xT = sb("xT", [P, NP])
        keyT = sb("keyT", [P, NP])
        kv = sb("kv", [P, NT, KV])
        srow = sb("srow", [P, 2, NP])
        gath = sb("gath", [P, 2, TOP, KV])
        wh2a = sb("wh2a", [P, NP])
        Whx = sb("Whx", [P, NT, D + 1])
        simw = sb("simw", [P, H, PS, NK])
        Wqs = sb("Wqs", [P, H, D])
        Wos = sb("Wos", [P, H, D])
        wq_now = sb("wq_now", [P, D])
        wpk = sb("wpk", [DK, PS * H, D])
        kpk = sb("kpk", [DK, PS * H, NK])
        Wsb = sb("Wsb", [P, D + 1])
        WTs = sb("WTs", [P, D])
        asb = sb("asb", [P, 2])
        wa2 = sb("wa2", [P, P])
        ident = sb("ident", [P, P])
        identb = sb("identb", [P, P], bf16)
        future = sb("future", [P, P], bf16)
        iota16 = sb("iota16", [P, TOP])
        hoff = sb("hoff", [P, H])
        stat6 = sb("stat6", [P, 2, 6])
        stat2 = sb("stat2", [P, 2, 2])
        mv = sb("mv", [P, NT, 2])
        sd = sb("sd", [P, NT])
        rstd = sb("rstd", [P, NT])
        epsc = sb("epsc", [P, 1])
        hn = sb("hn", [P, 2, D])
        hTs = sb("hTs", [P, 2, P])
        gmax = sb("gmax", [P, 2])
        gneg = sb("gneg", [P, 2])
        gsum = sb("gsum", [P, 2])
        grec = sb("grec", [P, 2])
        prT = sb("prT", [P, 2, CH])
        sims = sb("sims", [P, 2, PS, NK])
        simr = sb("simr", [P, PS, NK])
        top = sb("top", [P, PS, TOP])
        topi = sb("topi", [P, PS, TOP], u32)
        cand = sb("cand", [P, TOP, TOP])
        candr = sb("candr", [P, TOP * TOP])
        fin = sb("fin", [P, 2, TOP])
        finp = sb("finp", [P, TOP], u32)
        finr = sb("finr", [P, PS, TOP], u32)
        hot = sb("hot", [P, PS, TOP, TOP])
        part = sb("part", [P, PS, TOP])
        rowf = sb("rowf", [P, TOP])
        rowi = sb("rowi", [P, 2, TOP], u32)
        fneg = sb("fneg", [P, 2])
        fexp = sb("fexp", [P, 2, TOP])
        fsum = sb("fsum", [P, 2])
        frec = sb("frec", [P, 2])
        wmix = sb("wmix", [P, 2, TOP])
        qT = sb("qT", [P, P])
        rneg = sb("rneg", [P, 2])
        rsum = sb("rsum", [P, 2])
        rrec = sb("rrec", [P, 2])
        oS = sb("oS", [P, D])
        oT = sb("oT", [P, P])

        adjs = gath[:, :, :, :].rearrange("p b k d -> p b (k d)").bitcast(i32)
        mneg = kv[:, :, :].rearrange("p t d -> p (t d)").rearrange("p (b n) -> p b n", b=2)
        hp = keyT[:, :].rearrange("p (t d) -> p t d", d=D)
        wh2b = xT

        psS = [bank("psS0"), bank("psS1")]
        psT = [bank("psT0"), bank("psT1")]
        psO = bank("psO")
        psQ = bank("psQ")
        psY = bank("psY")
        psM = bank("psM")
        psG = [psO, psQ]
        ps_q, ps_k = psQ[:, 0:P], psQ[:, P:2 * P]
        ps_ot, ps_y = psY[:, 0:P], psY[:, P:2 * P]

        s_dve = sem("dve_step")
        x_loaded = sem("x_loaded")
        x_padded = sem("x_padded")
        w_loaded = sem("w_loaded")
        pk_loaded = sem("pk_loaded")
        wqo_loaded = sem("wqo_loaded")
        pool_step = sem("pool_step")
        consts_ready = sem("consts_ready")
        wa_ps, wa_ready = sem("wa_ps"), sem("wa_ready")
        simw_ps, simw_ready = sem("simw_ps"), sem("simw_ready")
        var_ready, sd_ready = sem("var_ready"), sem("sd_ready")
        norm_ready, normT_ps, normT_ready = sem("norm_ready"), sem("normT_ps"), sem("normT_ready")
        wh_ps, wh_ready, wh2_ready = sem("wh_ps"), sem("wh_ready"), sem("wh2_ready")
        var2_ready, sd2_ready = sem("var2_ready"), sem("sd2_ready")
        norm2_ready, norm2T_ps, norm2T_ready = sem("norm2_ready"), sem("norm2T_ps"), sem("norm2T_ready")
        adj_loaded = [sem("adj_loaded0"), sem("adj_loaded1")]
        mask_ready, gneg_ready, gexp_ready = sem("mask_ready"), sem("gneg_ready"), sem("gexp_ready")
        g_tps, g_pT, g_pv, g_out = sem("g_tps"), sem("g_pT"), sem("g_pv"), sem("g_out")
        elu_in, elu_exp = sem("elu_in"), sem("elu_exp")
        sims_ps, sims_ready, top_done = sem("sims_ps"), sem("sims_ready"), sem("top_done")
        fin_ready, fexp_ready, rows_ready = sem("fin_ready"), sem("fexp_ready"), sem("rows_ready")
        gathered = [sem("gathered0"), sem("gathered1")]
        kv_ready, k_ps, k_ready = sem("kv_ready"), sem("k_ps"), sem("k_ready")
        wq_ready, q_ps, q_ready = sem("wq_ready"), sem("q_ps"), sem("q_ready")
        s_ps, s_ready, rneg_ready, p_ready = sem("s_ps"), sem("s_ready"), sem("rneg_ready"), sem("p_ready")
        t_ps, pT_ready, pv_done = sem("t_ps"), sem("pT_ready"), sem("pv_done")
        o_ready, ot_ps, ot_ready, y_ps, y_added = (
            sem("o_ready"), sem("ot_ps"), sem("ot_ready"), sem("y_ps"), sem("y_added"))
        stored = sem("stored")
        tick = {e: sem(f"tick_{e}") for e in ("pool", "dve", "act")}

        block = ctx.enter_context(nc.Block())

        def held(eng, name):
            eng.sem_inc(tick[name], 1)

        def every_tile(eng, body):
            with eng.Fori(0, NT // 2) as r:
                for q in range(2):
                    body(r * 2 + q, q)

        def graph_tiles(eng, body):
            body(0, 0, True)
            with eng.Fori(0, (NT - 2) // 2) as r:
                for q in range(2):
                    body(r * 2 + (q + 1), (q + 1) % 2, False)
            body(NT - 1, 1, False)

        def every_head(eng, body):
            with eng.Fori(0, H - 1) as h:
                body(h, False)
            body(H - 1, True)

        @block.sync
        def _(sp):
            full = NT - 1
            sp.dma_start(xs[:, 0:full, :], x[0:full * P, :].rearrange("(t p) d -> p t d", p=P)).then_inc(x_loaded, 16)
            sp.wait_ge(x_padded, 1)
            sp.dma_start(xs[0:SPLIT, full, :], x[full * P:full * P + SPLIT, :]).then_inc(x_loaded, 16)
            sp.dma_start(xs[SPLIT:REST, full, :], x[full * P + SPLIT:N, :]).then_inc(x_loaded, 16)
            sp.dma_start(Wsb[:, 0:D], W).then_inc(w_loaded, 16)
            sp.dma_start(WTs[:, :], WT).then_inc(w_loaded, 16)
            sp.dma_start(asb[:, :], a).then_inc(w_loaded, 16)

            def load_adj(i, q, rows):
                sp.dma_start(adjs[0:SPLIT, q, 0:N], adj[bass.ds(i * P, SPLIT), :]).then_inc(adj_loaded[q], 16)
                sp.dma_start(adjs[SPLIT:rows, q, 0:N], adj[bass.ds(i * P + SPLIT, rows - SPLIT), :])\
                    .then_inc(adj_loaded[q], 16)

            load_adj(0, 0, P)
            load_adj(1, 1, P)
            sp.dma_start(wpk[:, :, :], wqpkT.rearrange("s h k c -> k (s h) c")).then_inc(pk_loaded, 16)
            sp.dma_start(kpk[:, :, :], keysT.rearrange("s h k n -> k (s h) n")).then_inc(pk_loaded, 16)
            sp.dma_start(Wqs[:, :, :], Wq.rearrange("c (h d) -> c h d", h=H)).then_inc(wqo_loaded, 16)
            sp.dma_start(Wos[:, :, :], Wo.rearrange("(h d) n -> d h n", h=H)).then_inc(wqo_loaded, 16)
            with sp.Fori(1, NT // 2 - 1) as r:
                for q in range(2):
                    sp.wait_ge(mask_ready, r * 2 + (q - 1))
                    load_adj(r * 2 + q, q, P)
            sp.wait_ge(mask_ready, NT - 3)
            load_adj(NT - 2, 0, P)
            sp.wait_ge(mask_ready, NT - 2)
            load_adj(NT - 1, 1, REST)
            for t in range(NT):
                rows = P if t < full else REST
                sp.wait_ge(y_added, (H - 1) * NT + t + 1)
                if rows == P:
                    sp.dma_start(out[t * P:t * P + rows, :], xs[:, t, :]).then_inc(stored, 16)
                else:
                    sp.dma_start(out[t * P:t * P + SPLIT, :], xs[0:SPLIT, t, :]).then_inc(stored, 16)
                    sp.dma_start(out[t * P + SPLIT:N, :], xs[SPLIT:rows, t, :]).then_inc(stored, 16)
            sp.wait_ge(stored, 16 * (NT + (REST < P)))

        @block.gpsimd
        def _(pool):
            nc.gpsimd.memset(ident[:, :], 0.0).then_inc(pool_step, 1)
            nc.gpsimd.memset(future[:, :], 0.0).then_inc(pool_step, 1)
            nc.gpsimd.memset(epsc[:, :], EPS)
            nc.gpsimd.memset(srow[:, :, N:NP], 0.0)
            nc.gpsimd.iota(iota16[:, :], [[1, TOP]], base=0, channel_multiplier=0,
                           allow_small_or_imprecise_dtypes=True)
            nc.gpsimd.iota(hoff[:, :], [[NK * NK, H]], base=0, channel_multiplier=0,
                           allow_small_or_imprecise_dtypes=True)
            pool.wait_ge(pool_step, 2)
            nc.gpsimd.affine_select(out=ident[:, :], in_=ident[:, :], compare_op=ALU.not_equal, fill=1.0,
                                    base=0, pattern=[[-1, P]], channel_multiplier=1).then_inc(pool_step, 1)
            nc.gpsimd.affine_select(out=future[:, :], in_=future[:, :], compare_op=ALU.is_ge, fill=FUTURE,
                                    base=0, pattern=[[-1, P]], channel_multiplier=1).then_inc(pool_step, 1)
            pool.wait_ge(pool_step, 4)
            nc.gpsimd.tensor_copy(identb[:, :], ident[:, :]).then_inc(consts_ready, 1)

            def mask(i, q, first):
                pool.wait_ge(adj_loaded[q], (i + 2 - q) * 16)
                pool.wait_ge(gneg_ready, i + 1)
                held(pool, "pool")
                nc.gpsimd.tensor_scalar(mneg[:, q, 0:N], adjs[:, q, 0:N], 0.0, MASKED, ALU.is_le, ALU.mult)\
                    .then_inc(mask_ready, 1)

            graph_tiles(pool, mask)

            def head(h, last):
                for t in range(NT):
                    q = t % 2
                    pool.wait_ge(rows_ready, h * NT + (t + 1))
                    pool.wait_ge(kv_ready, h * NT + (t + 1))
                    if not last:
                        held(pool, "pool")
                    for k in range(TOP):
                        pool.indirect_dma_start(gath[:, q, k, :], None, kv_table,
                                                bass.IndirectOffsetOnAxis(ap=rowi[:, q, k:k + 1], axis=0))\
                            .then_inc(gathered[q], 16)

            every_head(pool, head)

        @block.tensor
        def _(pe):
            mm, tr = nc.tensor.matmul, nc.tensor.transpose
            pe.wait_ge(w_loaded, 48)
            mm(psM[:, 0:2], WTs[:, :], asb[:, :], start=True, stop=True).then_inc(wa_ps, 1)
            pe.wait_ge(consts_ready, 1)
            pe.wait_ge(wa_ready, 1)

            def norm_tile(i, q):
                pe.wait_ge(norm_ready, i + 1)
                pe.wait_ge(normT_ready, i + 1)
                tr(psT[q][:, 0:P], hn[:, q, :], ident[:, :]).then_inc(normT_ps, 1)
                pe.wait_ge(normT_ready, i + 3)
                pe.wait_ge(wh_ready, i + 1)
                pe.wait_ge(wh2_ready, i + 1)
                mm(psS[q][:, 0:D + 1], hTs[:, q, :], Wsb[:, :], start=True, stop=True)
                mm(psG[q][:, 0:P], wa2[:, :], hTs[:, q, :], start=True, stop=True).then_inc(wh_ps, 1)

            every_tile(pe, norm_tile)

            pe.wait_ge(pk_loaded, 32)
            for h in range(H):
                if h >= 2:
                    pe.wait_ge(simw_ready, h - 1)
                for s in range(PS):
                    last = mm(psT[h % 2][:, s * NK:(s + 1) * NK], wpk[:, s * H + h, :], kpk[:, s * H + h, :],
                              start=True, stop=True)
                last.then_inc(simw_ps, 1)
            pe.wait_ge(simw_ready, H)
            pe.wait_ge(wh_ready, NT + 2)

            def graph_row(i, q):
                pe.wait_ge(gexp_ready, i + 1)
                pe.wait_ge(g_out, i + 1)

                def turn(c):
                    pe.wait_ge(g_pT, i * GC + (c + 1))
                    for b in range(min(C, NT - C * c)):
                        last = tr(psT[turned[0] % 2][:, b * P:(b + 1) * P],
                                  srow[:, q, (C * c + b) * P:(C * c + b + 1) * P], ident[:, :])
                    last.then_inc(g_tps, 1)
                    turned[0] += 1

                turned = [(q * GC) % 2]
                turn(0)
                for c in range(GC):
                    if c + 1 < GC:
                        turn(c + 1)
                    pe.wait_ge(g_pT, i * GC + (c + 3))
                    for b in range(min(C, NT - C * c)):
                        j = C * c + b
                        last = mm(psG[q][:, 0:D], prT[:, (q * GC + c) % 2, b * P:(b + 1) * P], Whx[:, j, 0:D],
                                  start=(j == 0), stop=(j == NT - 1))
                    last.then_inc(g_pv, 1)

            every_tile(pe, graph_row)

            def norm2_tile(i, q):
                pe.wait_ge(norm2_ready, i + 1)
                pe.wait_ge(norm2T_ready, i + 1)
                tr(psT[q][:, 0:P], hn[:, q, :], ident[:, :]).then_inc(norm2T_ps, 1)

            every_tile(pe, norm2_tile)
            pe.wait_ge(norm2T_ready, NT + 2)

            def find_sims(h, n, t):
                mm(psM[:, 0:PS * NK], xT[:, t * P:(t + 1) * P],
                   simw[:, bass.ds(h, 1), :, :].rearrange("p o s k -> p (o s k)"), start=True, stop=True)\
                    .then_inc(sims_ps, 1)

            find_sims(0, 0, 0)
            pe.wait_ge(sims_ready, 1)
            find_sims(0, 1, 1)

            def head(h, last):
                def project(t):
                    pe.wait_ge(o_ready, h * NT + (t + 1))
                    tr(ps_ot, oS[:, :], ident[:, :]).then_inc(ot_ps, 1)

                def project2(t):
                    pe.wait_ge(ot_ready, h * NT + (t + 1))
                    mm(ps_y, oT[:, :], Wos[:, bass.ds(h, 1), :].rearrange("p o d -> p (o d)"),
                       start=True, stop=True).then_inc(y_ps, 1)

                for t in range(NT):
                    if not (last and t + 2 >= NT):
                        pe.wait_ge(sims_ready, h * NT + (t + 2))
                        find_sims(h + (t + 2) // NT, None, (t + 2) % NT)
                    if t == 0:
                        pe.wait_ge(wq_ready, h + 1)
                    mm(ps_q, wq_now[:, :], xT[:, t * P:(t + 1) * P], start=True, stop=True).then_inc(q_ps, 1)
                    pe.wait_ge(q_ready, h * NT + (t + 1))
                    pe.wait_ge(kv_ready, h * NT + (t + 3))
                    tr(ps_k, kv[:, t, 0:D], ident[:, :]).then_inc(k_ps, 1)
                    if t >= 1:
                        project(t - 1)
                    pe.wait_ge(k_ready, h * NT + (t + 1))
                    for c in range(chunks_of[t]):
                        g = chunk_at[t] + c
                        w = min(CH, (t + 1) * P - c * CH)
                        pe.wait_ge(s_ready, h * NCH + (g + 1))
                        diagonal = c == chunks_of[t] - 1
                        one = mm(psS[g % 2][:, 0:w], qT[:, :], keyT[:, c * CH:c * CH + w],
                                 start=True, stop=not diagonal)
                        if diagonal:
                            one = mm(psS[g % 2][:, w - P:w], identb[:, :], future[:, :], start=False, stop=True)
                        one.then_inc(s_ps, 1)
                    if t >= 1:
                        project2(t - 1)
                    pe.wait_ge(p_ready, h * NT + (t + 1))

                    def turn(c):
                        g = chunk_at[t] + c
                        pe.wait_ge(pT_ready, h * NCH + (g + 1))
                        for b in range(min(C, t + 1 - c * C)):
                            last_one = tr(psT[g % 2][:, b * P:(b + 1) * P],
                                          srow[:, t % 2, (c * C + b) * P:(c * C + b + 1) * P], ident[:, :])
                        last_one.then_inc(t_ps, 1)

                    turn(0)
                    for c in range(chunks_of[t]):
                        g = chunk_at[t] + c
                        if c + 1 < chunks_of[t]:
                            turn(c + 1)
                        pe.wait_ge(pT_ready, h * NCH + (g + 3))
                        for b in range(min(C, t + 1 - c * C)):
                            j = c * C + b
                            last_one = mm(psO[:, 0:D], prT[:, g % 2, b * P:(b + 1) * P], kv[:, j, D:KV],
                                          start=(j == 0), stop=(j == t))
                        last_one.then_inc(pv_done, 1)
                project(NT - 1)
                project2(NT - 1)

            every_head(pe, head)

        @block.scalar
        def _(act):
            def copy(dst, src):
                return nc.scalar.activation(dst, src, ACT.Copy)

            for room in (normT_ready, wh2_ready, norm2T_ready, s_ready, g_pT, pT_ready):
                act.sem_inc(room, 2)
            act.wait_ge(var_ready, 1)
            act.wait_ge(consts_ready, 1)
            nc.scalar.activation(sd[:, :], mv[:, :, 1], ACT.Sqrt, bias=epsc[:, 0:1]).then_inc(sd_ready, 1)

            def norm_tile(i, q):
                act.wait_ge(normT_ps, i + 1)
                copy(hTs[:, q, :], psT[q][:, 0:P]).then_inc(normT_ready, 1)
                act.wait_ge(wh_ps, i + 1)
                held(act, "act")
                nc.scalar.activation(wh2a[:, bass.ds(i * P, P)], psG[q][:, 0:P], ACT.Copy, scale=ALPHA)
                nc.scalar.activation(wh2b[:, bass.ds(i * P, P)], psG[q][:, 0:P], ACT.Copy, scale=1.0 - ALPHA)\
                    .then_inc(wh2_ready, 1)

            every_tile(act, norm_tile)
            for h in range(H):
                act.wait_ge(simw_ps, h + 1)
                copy(simw[:, h, :, :], psT[h % 2][:, 0:PS * NK].rearrange("p (s k) -> p s k", s=PS))\
                    .then_inc(simw_ready, 1)

            def graph_chunks(i, q):
                for c in range(GC):
                    act.wait_ge(g_pv, i * GC + (c + 1))
                    act.wait_ge(g_tps, i * GC + (c + 1))
                    w = min(C, NT - C * c) * P
                    copy(prT[:, (q * GC + c) % 2, 0:w], psT[(q * GC + c) % 2][:, 0:w]).then_inc(g_pT, 1)

            def graph_tile(i, q, first):
                act.wait_ge(gneg_ready, i + 3)
                nc.scalar.activation(srow[:, q, 0:N], srow[:, q, 0:N], ACT.Exp, bias=gneg[:, q:q + 1],
                                     accum_out=gsum[:, q:q + 1]).then_inc(gexp_ready, 1)
                if not first:
                    graph_chunks(i - 1, (q + 1) % 2)

            graph_tiles(act, graph_tile)
            graph_chunks(NT - 1, 1)
            act.wait_ge(elu_in, 1)
            nc.scalar.activation(srow[:, 0, :], srow[:, 0, :], ACT.Exp).then_inc(elu_exp, 1)
            act.wait_ge(var2_ready, 1)
            nc.scalar.activation(sd[:, :], mv[:, :, 1], ACT.Sqrt, bias=epsc[:, 0:1]).then_inc(sd2_ready, 1)

            def norm2_tile(i, q):
                act.wait_ge(norm2T_ps, i + 1)
                held(act, "act")
                copy(xT[:, bass.ds(i * P, P)], psT[q][:, 0:P]).then_inc(norm2T_ready, 1)

            every_tile(act, norm2_tile)

            def sims_out(n, q):
                act.wait_ge(sims_ps, n + 1)
                copy(sims[:, q, :, :], psM[:, 0:PS * NK].rearrange("p (s k) -> p s k", s=PS))\
                    .then_inc(sims_ready, 1)

            def weights(n, q):
                act.wait_ge(fin_ready, n + 1)
                nc.scalar.activation(fexp[:, q, :], fin[:, q, :], ACT.Exp, bias=fneg[:, q:q + 1],
                                     accum_out=fsum[:, q:q + 1]).then_inc(fexp_ready, 1)

            sims_out(0, 0)
            sims_out(1, 1)
            weights(0, 0)
            weights(1, 1)
            act.wait_ge(wqo_loaded, 32)

            def head(h, last):
                def attention_out(t):
                    act.wait_ge(ot_ps, h * NT + (t + 1))
                    copy(oT[:, :], ps_ot).then_inc(ot_ready, 1)

                if not last:
                    held(act, "act")
                copy(wq_now[:, :], Wqs[:, bass.ds(h, 1), :].rearrange("p o d -> p (o d)")).then_inc(wq_ready, 1)
                for t in range(NT):
                    q = t % 2
                    ahead = not (last and t + 2 >= NT)
                    if ahead:
                        act.wait_ge(top_done, h * NT + (t + 1))
                        sims_out(h * NT + (t + 2), q)
                    act.wait_ge(q_ps, h * NT + (t + 1))
                    nc.scalar.activation(qT[:, :], ps_q, ACT.Copy, scale=SCALE).then_inc(q_ready, 1)
                    act.wait_ge(k_ps, h * NT + (t + 1))
                    copy(keyT[:, t * P:(t + 1) * P], ps_k).then_inc(k_ready, 1)
                    if t >= 1:
                        attention_out(t - 1)
                    for c in range(chunks_of[t]):
                        g = chunk_at[t] + c
                        w = min(CH, (t + 1) * P - c * CH)
                        act.wait_ge(s_ps, h * NCH + (g + 1))
                        copy(srow[:, q, c * CH:c * CH + w], psS[g % 2][:, 0:w]).then_inc(s_ready, 1)
                    if ahead:
                        weights(h * NT + (t + 2), q)
                    act.wait_ge(rneg_ready, h * NT + (t + 1))
                    nc.scalar.activation(srow[:, q, 0:(t + 1) * P], srow[:, q, 0:(t + 1) * P], ACT.Exp,
                                         bias=rneg[:, q:q + 1], accum_out=rsum[:, q:q + 1]).then_inc(p_ready, 1)
                    for c in range(chunks_of[t]):
                        g = chunk_at[t] + c
                        w = min(CH, (t + 1) * P - c * CH)
                        act.wait_ge(pv_done, h * NCH + (g + 1))
                        act.wait_ge(t_ps, h * NCH + (g + 1))
                        copy(prT[:, g % 2, 0:w], psT[g % 2][:, 0:w]).then_inc(pT_ready, 1)
                attention_out(NT - 1)

            every_head(act, head)

        @block.vector
        def _(dve):
            v = nc.vector
            steps = [0]

            def step(ins):
                steps[0] += 1
                ins.then_inc(s_dve, 1)
                return steps[0]

            def need(k):
                dve.wait_ge(s_dve, k)

            def restart():
                dve.wait_ge(s_dve, steps[0])
                dve.sem_clear(s_dve)
                steps[0] = 0

            def loop_body(body, *args):
                steps[0] = 0
                body(*args)
                restart()

            for room in (wh_ready, gneg_ready, g_out, g_pv, kv_ready, pv_done):
                dve.sem_inc(room, 2)
            v.memset(xs[:, NT - 1, :], 0.0).then_inc(x_padded, 1)
            dve.wait_ge(wa_ps, 1)
            v.tensor_scalar(Wsb[:, D:D + 1], psM[:, 0:1], ALPHA - 1.0, None, ALU.mult)
            v.tensor_copy(wa2[:, :], psM[:, 1:2].to_broadcast([P, P])).then_inc(wa_ready, 1)
            dve.wait_ge(x_loaded, 48)

            def stats(i, q):
                a1 = step(v.bn_stats(stat6[:, q, :], xs[:, bass.ds(i, 1), :].rearrange("p o d -> p (o d)")))
                need(a1)
                a2 = step(v.bn_aggr(stat2[:, q, :], stat6[:, q, :]))
                need(a2)
                return step(v.tensor_copy(mv[:, bass.ds(i, 1), :].rearrange("p o d -> p (o d)"), stat2[:, q, :]))

            def all_stats(done):
                every_tile(dve, lambda i, q: loop_body(stats, i, q))
                v.tensor_copy(stat6[:, 0, 0:1], mv[:, NT - 1, 0:1]).then_inc(done, 1)

            def normalized(i, q):
                return v.tensor_scalar(hn[:, q, :], xs[:, bass.ds(i, 1), :].rearrange("p o d -> p (o d)"),
                                       mv[:, bass.ds(i, 1), 0:1].rearrange("p o d -> p (o d)"),
                                       rstd[:, bass.ds(i, 1)], ALU.subtract, ALU.mult)

            all_stats(var_ready)
            dve.wait_ge(sd_ready, 1)
            k = step(v.reciprocal(rstd[:, :], sd[:, :]))
            need(k)
            restart()

            def norm_tile(i, q):
                dve.wait_ge(normT_ready, i + 1)
                normalized(i, q).then_inc(norm_ready, 1)
                dve.wait_ge(wh_ps, i + 1)
                v.tensor_copy(Whx[:, bass.ds(i, 1), :].rearrange("p o d -> p (o d)"), psS[q][:, 0:D + 1])\
                    .then_inc(wh_ready, 1)

            every_tile(dve, norm_tile)

            dve.wait_ge(wh2_ready, NT + 2)

            def graph_out(i, q):
                dve.wait_ge(gexp_ready, i + 1)
                r = step(v.reciprocal(grec[:, q:q + 1], gsum[:, q:q + 1]))
                need(r)
                dve.wait_ge(g_pv, i * GC + (GC + 2))
                v.tensor_scalar(hp[:, bass.ds(i, 1), :].rearrange("p o d -> p (o d)"), psG[q][:, 0:D],
                                grec[:, q:q + 1], None, ALU.mult).then_inc(g_out, 1)

            def graph_tile(i, q, first):
                steps[0] = 0
                dve.wait_ge(g_out, i + 1)
                m = step(v.scalar_tensor_tensor(srow[:, q, 0:N], wh2b[:, 0:N],
                                                Whx[:, bass.ds(i, 1), D:D + 1].rearrange("p o d -> p (o d)"),
                                                wh2a[:, 0:N], ALU.max, ALU.add))
                dve.wait_ge(mask_ready, i + 1)
                held(dve, "dve")
                need(m)
                m = step(v.tensor_tensor_reduce(out=srow[:, q, 0:N], in0=srow[:, q, 0:N], in1=mneg[:, q, 0:N],
                                                scale=1.0, scalar=LOWEST, op0=ALU.add, op1=ALU.max,
                                                accum_out=gmax[:, q:q + 1]))
                need(m)
                v.tensor_scalar(gneg[:, q:q + 1], gmax[:, q:q + 1], -1.0, None, ALU.mult).then_inc(gneg_ready, 1)
                if not first:
                    graph_out(i - 1, (q + 1) % 2)
                restart()

            graph_tiles(dve, graph_tile)
            graph_out(NT - 1, 1)
            dve.wait_ge(g_out, NT + 2)
            hflat = hp[:, :, :].rearrange("p t d -> p (t d)")
            xflat = xs[:, :, :].rearrange("p t d -> p (t d)")
            v.tensor_scalar(srow[:, 0, :], hflat, 0.0, None, ALU.min).then_inc(elu_in, 1)
            k = step(v.scalar_tensor_tensor(xflat, hflat, 0.0, xflat, ALU.max, ALU.add))
            need(k)
            dve.wait_ge(elu_exp, 1)
            k = step(v.scalar_tensor_tensor(xflat, srow[:, 0, :], -1.0, xflat, ALU.add, ALU.add))
            need(k)
            restart()

            all_stats(var2_ready)
            dve.wait_ge(sd2_ready, 1)
            k = step(v.reciprocal(rstd[:, :], sd[:, :]))
            need(k)
            restart()

            def norm2_tile(i, q):
                dve.wait_ge(norm2T_ready, i + 1)
                normalized(i, q).then_inc(norm2_ready, 1)

            every_tile(dve, norm2_tile)

            def search(h, n, q, loop):
                dve.wait_ge(sims_ready, n + 1)
                if loop:
                    held(dve, "dve")
                first = [step(v.max(top[:, s, 0:8], sims[:, q, s, :])) for s in range(PS)]
                for s in range(PS):
                    need(first[s])
                    v.max_index(topi[:, s, 0:8], top[:, s, 0:8], sims[:, q, s, :])
                cut = []
                for s in range(PS):
                    cut.append(step(v.match_replace(simr[:, s, :], top[:, s, 0:8], sims[:, q, s, :], LOWEST)))
                second = []
                for s in range(PS):
                    need(cut[s])
                    second.append(step(v.max(top[:, s, 8:16], simr[:, s, :])))
                need(second[1])
                c1 = step(v.tensor_tensor(cand[:, :, :], top[:, 0, :].unsqueeze(2).to_broadcast([P, TOP, TOP]),
                                          top[:, 1, :].unsqueeze(1).to_broadcast([P, TOP, TOP]), ALU.add))
                for s in range(PS):
                    i2 = step(v.max_index(topi[:, s, 8:16], top[:, s, 8:16], simr[:, s, :]))
                need(i2)
                v.tensor_copy(rowf[:, 0:1], top[:, 0, 0:1]).then_inc(top_done, 1)
                flat = cand[:, :, :].rearrange("p a b -> p (a b)")
                need(c1)
                m1 = step(v.max(fin[:, q, 0:8], flat))
                need(m1)
                v.max_index(finp[:, 0:8], fin[:, q, 0:8], flat)
                r1 = step(v.match_replace(candr[:, :], fin[:, q, 0:8], flat, LOWEST))
                need(r1)
                m2 = step(v.max(fin[:, q, 8:16], candr[:, :]))
                need(m2)
                v.tensor_scalar(fneg[:, q:q + 1], fin[:, q, 0:1], -1.0, None, ALU.mult).then_inc(fin_ready, 1)
                p2 = step(v.max_index(finp[:, 8:16], fin[:, q, 8:16], candr[:, :]))
                need(p2)
                v.tensor_scalar(finr[:, 0, :], finp[:, :], 4, None, ALU.logical_shift_right)
                d2 = step(v.tensor_scalar(finr[:, 1, :], finp[:, :], TOP - 1, None, ALU.bitwise_and))
                need(d2)
                for s in range(PS):
                    e1 = step(v.tensor_tensor(hot[:, s, :, :],
                                              finr[:, s, :].unsqueeze(2).to_broadcast([P, TOP, TOP]),
                                              iota16[:, :].unsqueeze(1).to_broadcast([P, TOP, TOP]),
                                              ALU.is_equal))
                need(e1)
                for s in range(PS):
                    e2 = step(v.tensor_tensor(hot[:, s, :, :], hot[:, s, :, :],
                                              topi[:, s, :].unsqueeze(1).to_broadcast([P, TOP, TOP]), ALU.mult))
                need(e2)
                e3 = step(v.tensor_reduce(part[:, :, :].rearrange("p s k -> p (s k)"),
                                          hot[:, :, :, :].rearrange("p s k r -> p (s k) r"), AX.X, ALU.add))
                need(e3)
                e4 = step(v.scalar_tensor_tensor(rowf[:, :], part[:, 1, :], float(NK), part[:, 0, :],
                                                 ALU.mult, ALU.add))
                need(e4)
                v.tensor_scalar(rowi[:, q, :], rowf[:, :], hoff[:, bass.ds(h, 1)], None, ALU.add)\
                    .then_inc(rows_ready, 1)
                dve.wait_ge(fexp_ready, n + 1)
                e5 = step(v.reciprocal(frec[:, q:q + 1], fsum[:, q:q + 1]))
                need(e5)
                step(v.tensor_scalar(wmix[:, q, :], fexp[:, q, :], frec[:, q:q + 1], None, ALU.mult))

            search(0, 0, 0, False)
            search(0, 1, 1, False)
            restart()

            def head(h, last):
                def mixture(t):
                    q = t % 2
                    dve.wait_ge(gathered[q], h * (16 * TOP * NT // 2) + 16 * TOP * (t // 2 + 1))
                    dst = kv[:, t, :]
                    m = step(v.tensor_scalar(dst, gath[:, q, 0, :], wmix[:, q, 0:1], None, ALU.mult))
                    for k in range(1, TOP):
                        need(m)
                        ins = v.scalar_tensor_tensor(dst, gath[:, q, k, :], wmix[:, q, k:k + 1], dst,
                                                     ALU.mult, ALU.add)
                        if k < TOP - 1:
                            m = step(ins)
                    ins.then_inc(kv_ready, 1)

                def attention(t):
                    q = t % 2
                    r = step(v.reciprocal(rrec[:, q:q + 1], rsum[:, q:q + 1]))
                    need(r)
                    v.tensor_scalar(oS[:, :], psO[:, 0:D], rrec[:, q:q + 1], None, ALU.mult).then_inc(o_ready, 1)

                def wait_pv(t):
                    dve.wait_ge(pv_done, h * NCH + (chunk_at[t + 1] + 2))

                def add(t):
                    dve.wait_ge(y_ps, h * NT + (t + 1))
                    v.tensor_tensor(xs[:, t, :], xs[:, t, :], ps_y, ALU.add).then_inc(y_added, 1)

                steps[0] = 0
                for t in range(NT):
                    q = t % 2
                    mixture(t)
                    if t >= 1:
                        wait_pv(t - 1)
                        attention(t - 1)
                    if not (last and t + 2 >= NT):
                        search(h + (t + 2) // NT, h * NT + (t + 2), q, not last)
                    if t >= 1:
                        add(t - 1)
                    dve.wait_ge(s_ready, h * NCH + (chunk_at[t + 1] + 2))
                    v.tensor_reduce(rneg[:, q:q + 1], srow[:, q, 0:(t + 1) * P], AX.X, ALU.max, negate=True)\
                        .then_inc(rneg_ready, 1)
                wait_pv(NT - 1)
                attention(NT - 1)
                add(NT - 1)
                restart()

            every_head(dve, head)


def kernel(x, adj, L0_gnn_W, L0_gnn_a, L0_ffn_Wq_pk, L0_ffn_pk_keys, L0_ffn_Wq, L0_ffn_keys_table,
           L0_ffn_values_table, L0_ffn_Wo):
    import numpy as np
    import concourse.bacc as bacc
    from concourse import mybir
    from concourse.bass_utils import run_bass_kernel_spmd

    parts, keys, heads, width = L0_ffn_pk_keys.shape
    dim = x.shape[1]
    arrays = {
        "x": x,
        "adj": adj,
        "W": L0_gnn_W,
        "WT": np.asarray(L0_gnn_W).T,
        "a": np.asarray(L0_gnn_a).reshape(2, dim).T,
        "wqpkT": np.asarray(L0_ffn_Wq_pk).T.reshape(parts, heads, width, dim),
        "keysT": np.asarray(L0_ffn_pk_keys).transpose(0, 2, 3, 1),
        "Wq": L0_ffn_Wq,
        "kv_table": np.concatenate([np.asarray(L0_ffn_keys_table), np.asarray(L0_ffn_values_table)], axis=1),
        "Wo": L0_ffn_Wo,
    }
    nc = bacc.Bacc("TRN2", target_bir_lowering=False, num_devices=1)
    ins, args = {}, []
    for name, value in arrays.items():
        value = np.ascontiguousarray(value)
        ins[f"in_{name}"] = value
        args.append(nc.dram_tensor(f"in_{name}", value.shape, mybir.dt.from_np(value.dtype), kind="ExternalInput").ap())
    args.append(nc.dram_tensor("out_x", tuple(x.shape), mybir.dt.from_np(np.dtype("float32")), kind="ExternalOutput").ap())
    gat_then_product_key_attention(nc, *args)
    run = run_bass_kernel_spmd(nc, [ins], core_ids=[0])
    return run.results[0]["out_x"]
```

```python
import concourse.bass as bass
from concourse import mybir
from contextlib import ExitStack


def gat_then_product_key_attention(nc, x, adj, W, WT, a, wqpkT, keysT, Wq, kv_table, Wo, out):
    f32, bf16, u32, i32 = mybir.dt.float32, mybir.dt.bfloat16, mybir.dt.uint32, mybir.dt.int32
    ALU = mybir.AluOpType
    ACT = mybir.ActivationFunctionType
    AX = mybir.AxisListType

    P = 128
    N, D = x.shape
    NT = -(-N // P)
    NP = NT * P
    REST = N - (NT - 1) * P
    PS, H, DK, NK = keysT.shape
    TOP = 16
    C = 4
    CH = C * P
    ALPHA = 0.2
    MASKED = -9000000000000000.0
    FUTURE = -1e30
    LOWEST = -3.4028234663852886e38
    EPS = 1e-5
    SCALE = float(D) ** -0.5
    KV = 2 * D
    chunks_of = [-(-(t + 1) // C) for t in range(NT)]
    chunk_at = [sum(chunks_of[:t]) for t in range(NT + 1)]
    NCH = chunk_at[NT]
    GC = -(-NT // C)
    assert D == P and NK == P and PS == 2 and NT % 2 == 0 and NCH % 2 == 0 and NT >= 4 and GC % 2 == 1
    SPLIT = (REST // 16) * 16

    ctx = ExitStack()
    with ctx:
        def sb(name, shape, dt=f32):
            return ctx.enter_context(nc.sbuf_tensor(name, shape, dt))

        def bank(name):
            return ctx.enter_context(nc.psum_tensor(name, [P, 512], f32))

        def sem(name):
            return ctx.enter_context(nc.semaphore(name))

        xs = sb("xs", [P, NT, D])
        xT = sb("xT", [P, NP])
        keyT = sb("keyT", [P, NP])
        val = sb("val", [P, NT, D])
        kvm = sb("kvm", [P, 2, KV])
        srow = sb("srow", [P, NP])
        prow = sb("prow", [P, 2, NP])
        gath = sb("gath", [P, 2, TOP, KV])
        wh2a = sb("wh2a", [P, NP])
        Whx = sb("Whx", [P, NT, D + 1])
        simw = sb("simw", [P, H, PS, NK])
        Wqs = sb("Wqs", [P, H, D])
        Wos = sb("Wos", [P, H, D])
        wq_now = sb("wq_now", [P, D])
        wpk = sb("wpk", [DK, PS * H, D])
        kpk = sb("kpk", [DK, PS * H, NK])
        Wsb = sb("Wsb", [P, D + 1])
        WTs = sb("WTs", [P, D])
        asb = sb("asb", [P, 2])
        wa2 = sb("wa2", [P, P])
        ident = sb("ident", [P, P])
        identb = sb("identb", [P, P], bf16)
        future = sb("future", [P, P], bf16)
        iota16 = sb("iota16", [P, TOP])
        hoff = sb("hoff", [P, H])
        stat6 = sb("stat6", [P, 2, 6])
        stat2 = sb("stat2", [P, 2, 2])
        mv = sb("mv", [P, NT, 2])
        sd = sb("sd", [P, NT])
        rstd = sb("rstd", [P, NT])
        epsc = sb("epsc", [P, 1])
        hn = sb("hn", [P, 2, D])
        hTs = sb("hTs", [P, 2, P])
        gmax = sb("gmax", [P, 2])
        gneg = sb("gneg", [P, 2])
        gsum = sb("gsum", [P, 2])
        grec = sb("grec", [P, 2])
        prT = sb("prT", [P, 2, CH])
        sims = sb("sims", [P, 2, PS, NK])
        simr = sb("simr", [P, PS, NK])
        top = sb("top", [P, PS, TOP])
        topi = sb("topi", [P, PS, TOP], u32)
        cand = sb("cand", [P, TOP, TOP])
        candr = sb("candr", [P, TOP * TOP])
        fin = sb("fin", [P, 2, TOP])
        finp = sb("finp", [P, TOP], u32)
        finr = sb("finr", [P, PS, TOP], u32)
        hot = sb("hot", [P, PS, TOP, TOP])
        part = sb("part", [P, PS, TOP])
        rowf = sb("rowf", [P, TOP])
        rowi = sb("rowi", [P, 2, TOP], u32)
        fneg = sb("fneg", [P, 2])
        fexp = sb("fexp", [P, 2, TOP])
        fsum = sb("fsum", [P, 2])
        frec = sb("frec", [P, 2])
        wmix = sb("wmix", [P, 2, TOP])
        qT = sb("qT", [P, P])
        rneg = sb("rneg", [P, 2])
        rsum = sb("rsum", [P, 2])
        rrec = sb("rrec", [P, 2])
        oS = sb("oS", [P, D])
        oT = sb("oT", [P, P])

        adjs = gath[:, :, :, :].rearrange("p b k d -> p b (k d)").bitcast(i32)
        mneg = [val[:, :, :].rearrange("p t d -> p (t d)"), srow[:, :]]
        hp = keyT[:, :].rearrange("p (t d) -> p t d", d=D)
        wh2b = xT

        psS = [bank("psS0"), bank("psS1")]
        psT = [bank("psT0"), bank("psT1")]
        psO = bank("psO")
        psQ = bank("psQ")
        psY = bank("psY")
        psM = bank("psM")
        psG = [psO, psQ]
        ps_q, ps_k = psQ[:, 0:P], psQ[:, P:2 * P]
        ps_ot, ps_y = psY[:, 0:P], psY[:, P:2 * P]

        s_dve = sem("dve_step")
        x_loaded = sem("x_loaded")
        x_padded = sem("x_padded")
        w_loaded = sem("w_loaded")
        pk_loaded = sem("pk_loaded")
        wqo_loaded = sem("wqo_loaded")
        pool_step = sem("pool_step")
        consts_ready = sem("consts_ready")
        wa_ps, wa_ready = sem("wa_ps"), sem("wa_ready")
        simw_ps, simw_ready = sem("simw_ps"), sem("simw_ready")
        var_ready, sd_ready = sem("var_ready"), sem("sd_ready")
        norm_ready, normT_ps, normT_ready = sem("norm_ready"), sem("normT_ps"), sem("normT_ready")
        wh_ps, wh_ready, wh2_ready = sem("wh_ps"), sem("wh_ready"), sem("wh2_ready")
        var2_ready, sd2_ready = sem("var2_ready"), sem("sd2_ready")
        norm2_ready, norm2T_ps, norm2T_ready = sem("norm2_ready"), sem("norm2T_ps"), sem("norm2T_ready")
        adj_loaded = [sem("adj_loaded0"), sem("adj_loaded1")]
        mask_ready, gneg_ready, gexp_ready = sem("mask_ready"), sem("gneg_ready"), sem("gexp_ready")
        g_tps, g_pT, g_pv, g_out = sem("g_tps"), sem("g_pT"), sem("g_pv"), sem("g_out")
        elu_in, elu_exp = sem("elu_in"), sem("elu_exp")
        sims_ps, sims_ready, top_done = sem("sims_ps"), sem("sims_ready"), sem("top_done")
        fin_ready, fexp_ready, rows_ready = sem("fin_ready"), sem("fexp_ready"), sem("rows_ready")
        gathered = [sem("gathered0"), sem("gathered1")]
        kv_ready, k_ps, k_ready, v_ready = sem("kv_ready"), sem("k_ps"), sem("k_ready"), sem("v_ready")
        wq_ready, q_ps, q_ready = sem("wq_ready"), sem("q_ps"), sem("q_ready")
        s_ps, s_ready, rneg_ready, p_ready = sem("s_ps"), sem("s_ready"), sem("rneg_ready"), sem("p_ready")
        t_ps, pT_ready, pv_done = sem("t_ps"), sem("pT_ready"), sem("pv_done")
        o_ready, ot_ps, ot_ready, y_ps, y_added = (
            sem("o_ready"), sem("ot_ps"), sem("ot_ready"), sem("y_ps"), sem("y_added"))
        stored = sem("stored")
        tick = {e: sem(f"tick_{e}") for e in ("pool", "dve", "act")}

        block = ctx.enter_context(nc.Block())

        def held(eng, name):
            eng.sem_inc(tick[name], 1)

        def every_tile(eng, body):
            with eng.Fori(0, NT // 2) as r:
                for q in range(2):
                    body(r * 2 + q, q)

        def graph_tiles(eng, body):
            body(0, 0, True)
            with eng.Fori(0, (NT - 2) // 2) as r:
                for q in range(2):
                    body(r * 2 + (q + 1), (q + 1) % 2, False)
            body(NT - 1, 1, False)

        def every_head(eng, body):
            body(0, True, False)
            with eng.Fori(1, H - 1) as h:
                body(h, False, False)
            body(H - 1, False, True)

        def steps_of(first, last):
            for t in range(NT + 3 if last else NT):
                yield t, lambda d, t=t: not (first and t + d < 0) and not (last and t + d >= NT)

        def chunk0(t):
            return chunk_at[t % NT] + (t // NT) * NCH

        @block.sync
        def _(sp):
            full = NT - 1
            sp.dma_start(xs[:, 0:full, :], x[0:full * P, :].rearrange("(t p) d -> p t d", p=P)).then_inc(x_loaded, 16)
            sp.wait_ge(x_padded, 1)
            sp.dma_start(xs[0:SPLIT, full, :], x[full * P:full * P + SPLIT, :]).then_inc(x_loaded, 16)
            sp.dma_start(xs[SPLIT:REST, full, :], x[full * P + SPLIT:N, :]).then_inc(x_loaded, 16)
            sp.dma_start(Wsb[:, 0:D], W).then_inc(w_loaded, 16)
            sp.dma_start(WTs[:, :], WT).then_inc(w_loaded, 16)
            sp.dma_start(asb[:, :], a).then_inc(w_loaded, 16)

            def load_adj(i, q, rows):
                sp.dma_start(adjs[0:SPLIT, q, 0:N], adj[bass.ds(i * P, SPLIT), :]).then_inc(adj_loaded[q], 16)
                sp.dma_start(adjs[SPLIT:rows, q, 0:N], adj[bass.ds(i * P + SPLIT, rows - SPLIT), :])\
                    .then_inc(adj_loaded[q], 16)

            load_adj(0, 0, P)
            load_adj(1, 1, P)
            sp.dma_start(wpk[:, :, :], wqpkT.rearrange("s h k c -> k (s h) c")).then_inc(pk_loaded, 16)
            sp.dma_start(kpk[:, :, :], keysT.rearrange("s h k n -> k (s h) n")).then_inc(pk_loaded, 16)
            sp.dma_start(Wqs[:, :, :], Wq.rearrange("c (h d) -> c h d", h=H)).then_inc(wqo_loaded, 16)
            sp.dma_start(Wos[:, :, :], Wo.rearrange("(h d) n -> d h n", h=H)).then_inc(wqo_loaded, 16)
            with sp.Fori(1, NT // 2 - 1) as r:
                for q in range(2):
                    sp.wait_ge(mask_ready, r * 2 + (q - 1))
                    load_adj(r * 2 + q, q, P)
            sp.wait_ge(mask_ready, NT - 3)
            load_adj(NT - 2, 0, P)
            sp.wait_ge(mask_ready, NT - 2)
            load_adj(NT - 1, 1, REST)
            for t in range(NT):
                rows = P if t < full else REST
                sp.wait_ge(y_added, (H - 1) * NT + t + 1)
                if rows == P:
                    sp.dma_start(out[t * P:t * P + rows, :], xs[:, t, :]).then_inc(stored, 16)
                else:
                    sp.dma_start(out[t * P:t * P + SPLIT, :], xs[0:SPLIT, t, :]).then_inc(stored, 16)
                    sp.dma_start(out[t * P + SPLIT:N, :], xs[SPLIT:rows, t, :]).then_inc(stored, 16)
            sp.wait_ge(stored, 16 * (NT + (REST < P)))

        @block.gpsimd
        def _(pool):
            nc.gpsimd.memset(ident[:, :], 0.0).then_inc(pool_step, 1)
            nc.gpsimd.memset(future[:, :], 0.0).then_inc(pool_step, 1)
            nc.gpsimd.memset(epsc[:, :], EPS)
            nc.gpsimd.memset(prow[:, :, N:NP], 0.0)
            nc.gpsimd.iota(iota16[:, :], [[1, TOP]], base=0, channel_multiplier=0,
                           allow_small_or_imprecise_dtypes=True)
            nc.gpsimd.iota(hoff[:, :], [[NK * NK, H]], base=0, channel_multiplier=0,
                           allow_small_or_imprecise_dtypes=True)
            pool.wait_ge(pool_step, 2)
            nc.gpsimd.affine_select(out=ident[:, :], in_=ident[:, :], compare_op=ALU.not_equal, fill=1.0,
                                    base=0, pattern=[[-1, P]], channel_multiplier=1).then_inc(pool_step, 1)
            nc.gpsimd.affine_select(out=future[:, :], in_=future[:, :], compare_op=ALU.is_ge, fill=FUTURE,
                                    base=0, pattern=[[-1, P]], channel_multiplier=1).then_inc(pool_step, 1)
            pool.wait_ge(pool_step, 4)
            nc.gpsimd.tensor_copy(identb[:, :], ident[:, :]).then_inc(consts_ready, 1)

            def mask(i, q, first):
                pool.wait_ge(adj_loaded[q], (i + 2 - q) * 16)
                pool.wait_ge(gneg_ready, i + 1)
                held(pool, "pool")
                nc.gpsimd.tensor_scalar(mneg[q][:, 0:N], adjs[:, q, 0:N], 0.0, MASKED, ALU.is_le, ALU.mult)\
                    .then_inc(mask_ready, 1)

            graph_tiles(pool, mask)

            def head(h, first, last):
                for t in range(NT):
                    q = t % 2
                    pool.wait_ge(rows_ready, h * NT + (t + 1))
                    pool.wait_ge(kv_ready, h * NT + (t + 1))
                    held(pool, "pool")
                    for k in range(TOP):
                        pool.indirect_dma_start(gath[:, q, k, :], None, kv_table,
                                                bass.IndirectOffsetOnAxis(ap=rowi[:, q, k:k + 1], axis=0))\
                            .then_inc(gathered[q], 16)

            every_head(pool, head)

        @block.tensor
        def _(pe):
            mm, tr = nc.tensor.matmul, nc.tensor.transpose
            pe.wait_ge(w_loaded, 48)
            mm(psM[:, 0:2], WTs[:, :], asb[:, :], start=True, stop=True).then_inc(wa_ps, 1)
            pe.wait_ge(consts_ready, 1)
            pe.wait_ge(wa_ready, 1)

            def norm_tile(i, q):
                pe.wait_ge(norm_ready, i + 1)
                pe.wait_ge(normT_ready, i + 1)
                tr(psT[q][:, 0:P], hn[:, q, :], ident[:, :]).then_inc(normT_ps, 1)
                pe.wait_ge(normT_ready, i + 3)
                pe.wait_ge(wh_ready, i + 1)
                pe.wait_ge(wh2_ready, i + 1)
                mm(psS[q][:, 0:D + 1], hTs[:, q, :], Wsb[:, :], start=True, stop=True)
                mm(psG[q][:, 0:P], wa2[:, :], hTs[:, q, :], start=True, stop=True).then_inc(wh_ps, 1)

            every_tile(pe, norm_tile)

            pe.wait_ge(pk_loaded, 32)
            for h in range(H):
                if h >= 2:
                    pe.wait_ge(simw_ready, h - 1)
                for s in range(PS):
                    last = mm(psT[h % 2][:, s * NK:(s + 1) * NK], wpk[:, s * H + h, :], kpk[:, s * H + h, :],
                              start=True, stop=True)
                last.then_inc(simw_ps, 1)
            pe.wait_ge(simw_ready, H)
            pe.wait_ge(wh_ready, NT + 2)

            def graph_row(i, q):
                pe.wait_ge(gexp_ready, i + 1)
                pe.wait_ge(g_out, i + 1)

                def turn(c):
                    pe.wait_ge(g_pT, i * GC + (c + 1))
                    for b in range(min(C, NT - C * c)):
                        last = tr(psT[turned[0] % 2][:, b * P:(b + 1) * P],
                                  prow[:, q, (C * c + b) * P:(C * c + b + 1) * P], ident[:, :])
                    last.then_inc(g_tps, 1)
                    turned[0] += 1

                turned = [(q * GC) % 2]
                turn(0)
                for c in range(GC):
                    if c + 1 < GC:
                        turn(c + 1)
                    pe.wait_ge(g_pT, i * GC + (c + 3))
                    for b in range(min(C, NT - C * c)):
                        j = C * c + b
                        last = mm(psG[q][:, 0:D], prT[:, (q * GC + c) % 2, b * P:(b + 1) * P], Whx[:, j, 0:D],
                                  start=(j == 0), stop=(j == NT - 1))
                    last.then_inc(g_pv, 1)

            every_tile(pe, graph_row)

            def norm2_tile(i, q):
                pe.wait_ge(norm2_ready, i + 1)
                pe.wait_ge(norm2T_ready, i + 1)
                tr(psT[q][:, 0:P], hn[:, q, :], ident[:, :]).then_inc(norm2T_ps, 1)

            every_tile(pe, norm2_tile)
            pe.wait_ge(norm2T_ready, NT + 2)

            def find_sims(h, t):
                mm(psM[:, 0:PS * NK], xT[:, t * P:(t + 1) * P],
                   simw[:, bass.ds(h, 1), :, :].rearrange("p o s k -> p (o s k)"), start=True, stop=True)\
                    .then_inc(sims_ps, 1)

            for t in range(3):
                if t:
                    pe.wait_ge(sims_ready, t)
                find_sims(0, t)

            def head(h, first, last):
                def project(t):
                    pe.wait_ge(ot_ready, h * NT + (t + 1))
                    mm(ps_y, oT[:, :], Wos[:, bass.ds(h + t // NT, 1), :].rearrange("p o d -> p (o d)"),
                       start=True, stop=True).then_inc(y_ps, 1)

                def turn(t, c):
                    g = chunk0(t) + c
                    pe.wait_ge(pT_ready, h * NCH + (g + 1))
                    for b in range(min(C, t % NT + 1 - c * C)):
                        one = tr(psT[g % 2][:, b * P:(b + 1) * P],
                                 prow[:, t % 2, (c * C + b) * P:(c * C + b + 1) * P], ident[:, :])
                    one.then_inc(t_ps, 1)

                def attend(t):
                    pe.wait_ge(p_ready, h * NT + (t + 1))
                    pe.wait_ge(v_ready, h * NT + (t + 3))
                    n = chunks_of[t % NT]
                    turn(t, 0)
                    for c in range(n):
                        g = chunk0(t) + c
                        if c + 1 < n:
                            turn(t, c + 1)
                        pe.wait_ge(pT_ready, h * NCH + (g + 3))
                        for b in range(min(C, t % NT + 1 - c * C)):
                            j = c * C + b
                            one = mm(psO[:, 0:D], prT[:, g % 2, b * P:(b + 1) * P], val[:, j, :],
                                     start=(j == 0), stop=(j == t % NT))
                        one.then_inc(pv_done, 1)

                def score(t):
                    pe.wait_ge(q_ready, h * NT + (t + 1))
                    pe.wait_ge(kv_ready, h * NT + (t + 3))
                    tr(ps_k, kvm[:, t % 2, 0:D], ident[:, :]).then_inc(k_ps, 1)
                    pe.wait_ge(k_ready, h * NT + (t + 1))
                    for c in range(chunks_of[t]):
                        g = chunk0(t) + c
                        w = min(CH, (t + 1) * P - c * CH)
                        pe.wait_ge(s_ready, h * NCH + (g + 1))
                        diagonal = c == chunks_of[t] - 1
                        one = mm(psS[g % 2][:, 0:w], qT[:, :], keyT[:, c * CH:c * CH + w],
                                 start=True, stop=not diagonal)
                        if diagonal:
                            one = mm(psS[g % 2][:, w - P:w], identb[:, :], future[:, :], start=False, stop=True)
                        one.then_inc(s_ps, 1)

                for t, there in steps_of(first, last):
                    if there(-3):
                        project(t - 3)
                    if there(3):
                        pe.wait_ge(sims_ready, h * NT + (t + 3))
                        find_sims(h + (t + 3) // NT, (t + 3) % NT)
                    if there(0):
                        if t == 0:
                            pe.wait_ge(wq_ready, h + 1)
                        mm(ps_q, wq_now[:, :], xT[:, t * P:(t + 1) * P], start=True, stop=True).then_inc(q_ps, 1)
                    if there(-2):
                        attend(t - 2)
                    if there(0):
                        score(t)
                    if there(-2):
                        pe.wait_ge(o_ready, h * NT + (t - 1))
                        tr(ps_ot, oS[:, :], ident[:, :]).then_inc(ot_ps, 1)

            every_head(pe, head)

        @block.scalar
        def _(act):
            def copy(dst, src):
                return nc.scalar.activation(dst, src, ACT.Copy)

            for room in (normT_ready, wh2_ready, norm2T_ready, s_ready, g_pT, pT_ready, v_ready):
                act.sem_inc(room, 2)
            act.wait_ge(var_ready, 1)
            act.wait_ge(consts_ready, 1)
            nc.scalar.activation(sd[:, :], mv[:, :, 1], ACT.Sqrt, bias=epsc[:, 0:1]).then_inc(sd_ready, 1)

            def norm_tile(i, q):
                act.wait_ge(normT_ps, i + 1)
                copy(hTs[:, q, :], psT[q][:, 0:P]).then_inc(normT_ready, 1)
                act.wait_ge(wh_ps, i + 1)
                held(act, "act")
                nc.scalar.activation(wh2a[:, bass.ds(i * P, P)], psG[q][:, 0:P], ACT.Copy, scale=ALPHA)
                nc.scalar.activation(wh2b[:, bass.ds(i * P, P)], psG[q][:, 0:P], ACT.Copy, scale=1.0 - ALPHA)\
                    .then_inc(wh2_ready, 1)

            every_tile(act, norm_tile)
            for h in range(H):
                act.wait_ge(simw_ps, h + 1)
                copy(simw[:, h, :, :], psT[h % 2][:, 0:PS * NK].rearrange("p (s k) -> p s k", s=PS))\
                    .then_inc(simw_ready, 1)

            def graph_chunks(i, q):
                for c in range(GC):
                    act.wait_ge(g_pv, i * GC + (c + 1))
                    act.wait_ge(g_tps, i * GC + (c + 1))
                    w = min(C, NT - C * c) * P
                    copy(prT[:, (q * GC + c) % 2, 0:w], psT[(q * GC + c) % 2][:, 0:w]).then_inc(g_pT, 1)

            def graph_tile(i, q, first):
                act.wait_ge(gneg_ready, i + 3)
                nc.scalar.activation(prow[:, q, 0:N], prow[:, q, 0:N], ACT.Exp, bias=gneg[:, q:q + 1],
                                     accum_out=gsum[:, q:q + 1]).then_inc(gexp_ready, 1)
                if not first:
                    graph_chunks(i - 1, (q + 1) % 2)

            graph_tiles(act, graph_tile)
            graph_chunks(NT - 1, 1)
            act.wait_ge(elu_in, 1)
            nc.scalar.activation(prow[:, 0, :], prow[:, 0, :], ACT.Exp).then_inc(elu_exp, 1)
            act.wait_ge(var2_ready, 1)
            nc.scalar.activation(sd[:, :], mv[:, :, 1], ACT.Sqrt, bias=epsc[:, 0:1]).then_inc(sd2_ready, 1)

            def norm2_tile(i, q):
                act.wait_ge(norm2T_ps, i + 1)
                held(act, "act")
                copy(xT[:, bass.ds(i * P, P)], psT[q][:, 0:P]).then_inc(norm2T_ready, 1)

            every_tile(act, norm2_tile)

            def sims_out(n, q):
                act.wait_ge(sims_ps, n + 1)
                copy(sims[:, q, :, :], psM[:, 0:PS * NK].rearrange("p (s k) -> p s k", s=PS))\
                    .then_inc(sims_ready, 1)

            def weights(n, q):
                act.wait_ge(fin_ready, n + 1)
                nc.scalar.activation(fexp[:, q, :], fin[:, q, :], ACT.Exp, bias=fneg[:, q:q + 1],
                                     accum_out=fsum[:, q:q + 1]).then_inc(fexp_ready, 1)

            sims_out(0, 0)
            sims_out(1, 1)
            weights(0, 0)
            weights(1, 1)
            act.wait_ge(top_done, 1)
            sims_out(2, 0)
            act.wait_ge(wqo_loaded, 32)

            def head(h, first, last):
                if not (first or last):
                    held(act, "act")
                copy(wq_now[:, :], Wqs[:, bass.ds(h, 1), :].rearrange("p o d -> p (o d)")).then_inc(wq_ready, 1)
                for t, there in steps_of(first, last):
                    q = t % 2
                    if there(3):
                        act.wait_ge(top_done, h * NT + (t + 2))
                        sims_out(h * NT + (t + 3), 1 - q)
                    if there(0):
                        act.wait_ge(q_ps, h * NT + (t + 1))
                        nc.scalar.activation(qT[:, :], ps_q, ACT.Copy, scale=SCALE).then_inc(q_ready, 1)
                    if there(-2):
                        for c in range(chunks_of[(t - 2) % NT]):
                            g = chunk0(t - 2) + c
                            w = min(CH, ((t - 2) % NT + 1) * P - c * CH)
                            act.wait_ge(pv_done, h * NCH + (g + 1))
                            act.wait_ge(t_ps, h * NCH + (g + 1))
                            copy(prT[:, g % 2, 0:w], psT[g % 2][:, 0:w]).then_inc(pT_ready, 1)
                    if there(-1):
                        w = ((t - 1) % NT + 1) * P
                        act.wait_ge(rneg_ready, h * NT + t)
                        nc.scalar.activation(prow[:, 1 - q, 0:w], srow[:, 0:w], ACT.Exp,
                                             bias=rneg[:, 1 - q:2 - q], accum_out=rsum[:, 1 - q:2 - q])\
                            .then_inc(p_ready, 1)
                        act.wait_ge(pv_done, h * NCH + (chunk0(t - 1) + 2))
                        copy(val[:, (t - 1) % NT, :], kvm[:, 1 - q, D:KV]).then_inc(v_ready, 1)
                    if there(2):
                        weights(h * NT + (t + 2), q)
                    if there(0):
                        act.wait_ge(k_ps, h * NT + (t + 1))
                        copy(keyT[:, t * P:(t + 1) * P], ps_k).then_inc(k_ready, 1)
                        for c in range(chunks_of[t]):
                            g = chunk0(t) + c
                            w = min(CH, (t + 1) * P - c * CH)
                            act.wait_ge(s_ps, h * NCH + (g + 1))
                            copy(srow[:, c * CH:c * CH + w], psS[g % 2][:, 0:w]).then_inc(s_ready, 1)
                    if there(-2):
                        act.wait_ge(ot_ps, h * NT + (t - 1))
                        copy(oT[:, :], ps_ot).then_inc(ot_ready, 1)

            every_head(act, head)

        @block.vector
        def _(dve):
            v = nc.vector
            steps = [0]

            def step(ins):
                steps[0] += 1
                ins.then_inc(s_dve, 1)
                return steps[0]

            def need(k):
                dve.wait_ge(s_dve, k)

            def restart():
                dve.wait_ge(s_dve, steps[0])
                dve.sem_clear(s_dve)
                steps[0] = 0

            def loop_body(body, *args):
                steps[0] = 0
                body(*args)
                restart()

            for room in (wh_ready, gneg_ready, g_out, g_pv, kv_ready, pv_done):
                dve.sem_inc(room, 2)
            v.memset(xs[:, NT - 1, :], 0.0).then_inc(x_padded, 1)
            dve.wait_ge(wa_ps, 1)
            v.tensor_scalar(Wsb[:, D:D + 1], psM[:, 0:1], ALPHA - 1.0, None, ALU.mult)
            v.tensor_copy(wa2[:, :], psM[:, 1:2].to_broadcast([P, P])).then_inc(wa_ready, 1)
            dve.wait_ge(x_loaded, 48)

            def stats(i, q):
                a1 = step(v.bn_stats(stat6[:, q, :], xs[:, bass.ds(i, 1), :].rearrange("p o d -> p (o d)")))
                need(a1)
                a2 = step(v.bn_aggr(stat2[:, q, :], stat6[:, q, :]))
                need(a2)
                return step(v.tensor_copy(mv[:, bass.ds(i, 1), :].rearrange("p o d -> p (o d)"), stat2[:, q, :]))

            def all_stats(done):
                every_tile(dve, lambda i, q: loop_body(stats, i, q))
                v.tensor_copy(stat6[:, 0, 0:1], mv[:, NT - 1, 0:1]).then_inc(done, 1)

            def normalized(i, q):
                return v.tensor_scalar(hn[:, q, :], xs[:, bass.ds(i, 1), :].rearrange("p o d -> p (o d)"),
                                       mv[:, bass.ds(i, 1), 0:1].rearrange("p o d -> p (o d)"),
                                       rstd[:, bass.ds(i, 1)], ALU.subtract, ALU.mult)

            all_stats(var_ready)
            dve.wait_ge(sd_ready, 1)
            k = step(v.reciprocal(rstd[:, :], sd[:, :]))
            need(k)
            restart()

            def norm_tile(i, q):
                dve.wait_ge(normT_ready, i + 1)
                normalized(i, q).then_inc(norm_ready, 1)
                dve.wait_ge(wh_ps, i + 1)
                v.tensor_copy(Whx[:, bass.ds(i, 1), :].rearrange("p o d -> p (o d)"), psS[q][:, 0:D + 1])\
                    .then_inc(wh_ready, 1)

            every_tile(dve, norm_tile)

            dve.wait_ge(wh2_ready, NT + 2)

            def graph_out(i, q):
                dve.wait_ge(gexp_ready, i + 1)
                r = step(v.reciprocal(grec[:, q:q + 1], gsum[:, q:q + 1]))
                need(r)
                dve.wait_ge(g_pv, i * GC + (GC + 2))
                v.tensor_scalar(hp[:, bass.ds(i, 1), :].rearrange("p o d -> p (o d)"), psG[q][:, 0:D],
                                grec[:, q:q + 1], None, ALU.mult).then_inc(g_out, 1)

            def graph_tile(i, q, first):
                steps[0] = 0
                dve.wait_ge(g_out, i + 1)
                m = step(v.scalar_tensor_tensor(prow[:, q, 0:N], wh2b[:, 0:N],
                                                Whx[:, bass.ds(i, 1), D:D + 1].rearrange("p o d -> p (o d)"),
                                                wh2a[:, 0:N], ALU.max, ALU.add))
                dve.wait_ge(mask_ready, i + 1)
                held(dve, "dve")
                need(m)
                m = step(v.tensor_tensor_reduce(out=prow[:, q, 0:N], in0=prow[:, q, 0:N], in1=mneg[q][:, 0:N],
                                                scale=1.0, scalar=LOWEST, op0=ALU.add, op1=ALU.max,
                                                accum_out=gmax[:, q:q + 1]))
                need(m)
                v.tensor_scalar(gneg[:, q:q + 1], gmax[:, q:q + 1], -1.0, None, ALU.mult).then_inc(gneg_ready, 1)
                if not first:
                    graph_out(i - 1, (q + 1) % 2)
                restart()

            graph_tiles(dve, graph_tile)
            graph_out(NT - 1, 1)
            dve.wait_ge(g_out, NT + 2)
            hflat = hp[:, :, :].rearrange("p t d -> p (t d)")
            xflat = xs[:, :, :].rearrange("p t d -> p (t d)")
            v.tensor_scalar(prow[:, 0, :], hflat, 0.0, None, ALU.min).then_inc(elu_in, 1)
            k = step(v.scalar_tensor_tensor(xflat, hflat, 0.0, xflat, ALU.max, ALU.add))
            need(k)
            dve.wait_ge(elu_exp, 1)
            k = step(v.scalar_tensor_tensor(xflat, prow[:, 0, :], -1.0, xflat, ALU.add, ALU.add))
            need(k)
            restart()

            all_stats(var2_ready)
            dve.wait_ge(sd2_ready, 1)
            k = step(v.reciprocal(rstd[:, :], sd[:, :]))
            need(k)
            restart()

            def norm2_tile(i, q):
                dve.wait_ge(norm2T_ready, i + 1)
                normalized(i, q).then_inc(norm2_ready, 1)

            every_tile(dve, norm2_tile)

            def search(h, n, q, mix, largest):
                dve.wait_ge(sims_ready, n + 1)
                held(dve, "dve")
                part1 = [step(v.max(top[:, s, 0:8], sims[:, q, s, :])) for s in range(PS)]
                mix(5)
                need(part1[1])
                for s in range(PS):
                    cut = step(v.match_replace(simr[:, s, :], top[:, s, 0:8], sims[:, q, s, :], LOWEST))
                for s in range(PS):
                    i1 = step(v.max_index(topi[:, s, 0:8], top[:, s, 0:8], sims[:, q, s, :]))
                need(cut)
                part2 = [step(v.max(top[:, s, 8:16], simr[:, s, :])) for s in range(PS)]
                mix(6)
                need(i1)
                v.tensor_copy(rowf[:, 0:1], top[:, 0, 0:1]).then_inc(top_done, 1)
                need(part2[1])
                flat = cand[:, :, :].rearrange("p a b -> p (a b)")
                sums = step(v.tensor_tensor(cand[:, :, :], top[:, 0, :].unsqueeze(2).to_broadcast([P, TOP, TOP]),
                                            top[:, 1, :].unsqueeze(1).to_broadcast([P, TOP, TOP]), ALU.add))
                for s in range(PS):
                    i2 = step(v.max_index(topi[:, s, 8:16], top[:, s, 8:16], simr[:, s, :]))
                need(sums)
                f1 = step(v.max(fin[:, q, 0:8], flat))
                mix(7)
                need(f1)
                cut = step(v.match_replace(candr[:, :], fin[:, q, 0:8], flat, LOWEST))
                v.max_index(finp[:, 0:8], fin[:, q, 0:8], flat)
                need(cut)
                f2 = step(v.max(fin[:, q, 8:16], candr[:, :]))
                mix(8)
                v.tensor_scalar(fneg[:, q:q + 1], fin[:, q, 0:1], -1.0, None, ALU.mult).then_inc(fin_ready, 1)
                need(f2)
                p2 = step(v.max_index(finp[:, 8:16], fin[:, q, 8:16], candr[:, :]))
                mix(9)
                need(p2)
                v.tensor_scalar(finr[:, 0, :], finp[:, :], 4, None, ALU.logical_shift_right)
                ranks = step(v.tensor_scalar(finr[:, 1, :], finp[:, :], TOP - 1, None, ALU.bitwise_and))
                mix(10)
                largest()
                need(ranks)
                for s in range(PS):
                    hot1 = step(v.tensor_tensor(hot[:, s, :, :],
                                                finr[:, s, :].unsqueeze(2).to_broadcast([P, TOP, TOP]),
                                                iota16[:, :].unsqueeze(1).to_broadcast([P, TOP, TOP]),
                                                ALU.is_equal))
                mix(11)
                need(hot1)
                need(i2)
                for s in range(PS):
                    hot2 = step(v.tensor_tensor(hot[:, s, :, :], hot[:, s, :, :],
                                                topi[:, s, :].unsqueeze(1).to_broadcast([P, TOP, TOP]), ALU.mult))
                mix(12)
                need(hot2)
                keys = step(v.tensor_reduce(part[:, :, :].rearrange("p s k -> p (s k)"),
                                            hot[:, :, :, :].rearrange("p s k r -> p (s k) r"), AX.X, ALU.add))
                mix(13)
                need(keys)
                rows = step(v.scalar_tensor_tensor(rowf[:, :], part[:, 1, :], float(NK), part[:, 0, :],
                                                   ALU.mult, ALU.add))
                mix(14)
                need(rows)
                v.tensor_scalar(rowi[:, q, :], rowf[:, :], hoff[:, bass.ds(h, 1)], None, ALU.add)\
                    .then_inc(rows_ready, 1)
                mix(15)

            def weigh1(n, q):
                dve.wait_ge(fexp_ready, n + 1)
                return step(v.reciprocal(frec[:, q:q + 1], fsum[:, q:q + 1]))

            def weigh2(r, q):
                need(r)
                return step(v.tensor_scalar(wmix[:, q, :], fexp[:, q, :], frec[:, q:q + 1], None, ALU.mult))

            def nothing(*_):
                pass

            search(0, 0, 0, nothing, nothing)
            search(0, 1, 1, nothing, nothing)
            weigh2(weigh1(0, 0), 0)
            restart()

            def head(h, first, last):
                steps[0] = 0
                for t, there in steps_of(first, last):
                    q = t % 2
                    done = [0]

                    def mix(k):
                        if not there(0):
                            return
                        dst = kvm[:, q, :]
                        if k == 0:
                            dve.wait_ge(gathered[q], h * (16 * TOP * NT // 2) + 16 * TOP * (t // 2 + 1))
                            dve.wait_ge(v_ready, h * NT + (t + 1))
                            done[0] = step(v.tensor_scalar(dst, gath[:, q, 0, :], wmix[:, q, 0:1], None, ALU.mult))
                            return
                        need(done[0])
                        one = v.scalar_tensor_tensor(dst, gath[:, q, k, :], wmix[:, q, k:k + 1], dst,
                                                     ALU.mult, ALU.add)
                        if k < TOP - 1:
                            done[0] = step(one)
                        else:
                            one.then_inc(kv_ready, 1)

                    mix(0)
                    if there(1):
                        r = weigh1(h * NT + (t + 1), 1 - q)
                    mix(1)
                    if there(1):
                        weigh2(r, 1 - q)
                    mix(2)
                    mix(3)
                    mix(4)

                    def largest():
                        if there(-1):
                            dve.wait_ge(s_ready, h * NCH + (chunk0(t) + 2))
                            v.tensor_reduce(rneg[:, 1 - q:2 - q], srow[:, 0:((t - 1) % NT + 1) * P], AX.X,
                                            ALU.max, negate=True).then_inc(rneg_ready, 1)

                    if there(2):
                        search(h + (t + 2) // NT, h * NT + (t + 2), q, mix, largest)
                    else:
                        for k in range(5, TOP):
                            mix(k)
                        largest()
                    if there(-3):
                        dve.wait_ge(y_ps, h * NT + (t - 2))
                        u = (t - 3) % NT
                        v.tensor_tensor(xs[:, u, :], xs[:, u, :], ps_y, ALU.add).then_inc(y_added, 1)
                    if there(-2):
                        dve.wait_ge(p_ready, h * NT + (t - 1))
                        r = step(v.reciprocal(rrec[:, q:q + 1], rsum[:, q:q + 1]))
                        dve.wait_ge(pv_done, h * NCH + (chunk0(t - 1) + 2))
                        need(r)
                        v.tensor_scalar(oS[:, :], psO[:, 0:D], rrec[:, q:q + 1], None, ALU.mult).then_inc(o_ready, 1)
                restart()

            every_head(dve, head)


def kernel(x, adj, L0_gnn_W, L0_gnn_a, L0_ffn_Wq_pk, L0_ffn_pk_keys, L0_ffn_Wq, L0_ffn_keys_table,
           L0_ffn_values_table, L0_ffn_Wo):
    import numpy as np
    import concourse.bacc as bacc
    from concourse import mybir
    from concourse.bass_utils import run_bass_kernel_spmd

    parts, keys, heads, width = L0_ffn_pk_keys.shape
    dim = x.shape[1]
    arrays = {
        "x": x,
        "adj": adj,
        "W": L0_gnn_W,
        "WT": np.asarray(L0_gnn_W).T,
        "a": np.asarray(L0_gnn_a).reshape(2, dim).T,
        "wqpkT": np.asarray(L0_ffn_Wq_pk).T.reshape(parts, heads, width, dim),
        "keysT": np.asarray(L0_ffn_pk_keys).transpose(0, 2, 3, 1),
        "Wq": L0_ffn_Wq,
        "kv_table": np.concatenate([np.asarray(L0_ffn_keys_table), np.asarray(L0_ffn_values_table)], axis=1),
        "Wo": L0_ffn_Wo,
    }
    nc = bacc.Bacc("TRN2", target_bir_lowering=False, num_devices=1)
    ins, args = {}, []
    for name, value in arrays.items():
        value = np.ascontiguousarray(value)
        ins[f"in_{name}"] = value
        args.append(nc.dram_tensor(f"in_{name}", value.shape, mybir.dt.from_np(value.dtype), kind="ExternalInput").ap())
    args.append(nc.dram_tensor("out_x", tuple(x.shape), mybir.dt.from_np(np.dtype("float32")), kind="ExternalOutput").ap())
    gat_then_product_key_attention(nc, *args)
    run = run_bass_kernel_spmd(nc, [ins], core_ids=[0])
    return run.results[0]["out_x"]
```

```python
import concourse.bass as bass
from concourse import mybir
from contextlib import ExitStack


def gat_then_product_key_attention(nc, x, adj, W, WT, a, wqpkT, keysT, Wq, kv_table, Wo, out):
    f32, bf16, u32, i32 = mybir.dt.float32, mybir.dt.bfloat16, mybir.dt.uint32, mybir.dt.int32
    ALU = mybir.AluOpType
    ACT = mybir.ActivationFunctionType
    AX = mybir.AxisListType

    P = 128
    N, D = x.shape
    NT = -(-N // P)
    NP = NT * P
    REST = N - (NT - 1) * P
    FIRST = 4
    PS, H, DK, NK = keysT.shape
    TOP = 16
    GROUP = 4
    C = 4
    CH = C * P
    ALPHA = 0.2
    MASKED = -9000000000000000.0
    FUTURE = -1e30
    LOWEST = -3.4028234663852886e38
    EPS = 1e-5
    SCALE = float(D) ** -0.5
    KV = 2 * D
    LONG = 4
    chunks_of = [-(-(t + 1) // C) for t in range(NT)]
    chunk_at = [sum(chunks_of[:t]) for t in range(NT + 1)]
    NCH = chunk_at[NT]
    GC = -(-NT // C)
    assert D == P and NK == P and PS == 2 and NT % 2 == 0 and NCH % 2 == 0 and NT >= 4 and GC % 2 == 1
    SPLIT = (REST // 16) * 16

    ctx = ExitStack()
    with ctx:
        def sb(name, shape, dt=f32):
            return ctx.enter_context(nc.sbuf_tensor(name, shape, dt))

        def bank(name):
            return ctx.enter_context(nc.psum_tensor(name, [P, 512], f32))

        def sem(name):
            return ctx.enter_context(nc.semaphore(name))

        xs = sb("xs", [P, NT, D])
        xT = sb("xT", [P, NP])
        keyT = sb("keyT", [P, NP])
        val = sb("val", [P, NT, D])
        kvm = sb("kvm", [P, 2, KV])
        srow = sb("srow", [P, NP])
        prow = sb("prow", [P, 2, NP])
        gath = sb("gath", [P, 2, TOP, KV])
        wh2a = sb("wh2a", [P, NP])
        Whx = sb("Whx", [P, NT, D + 1])
        simw = sb("simw", [P, H, PS, NK])
        Wqs = sb("Wqs", [P, H, D])
        Wos = sb("Wos", [P, H, D])
        wq_now = sb("wq_now", [P, D])
        wpk = sb("wpk", [DK, PS * H, D])
        kpk = sb("kpk", [DK, PS * H, NK])
        Wsb = sb("Wsb", [P, D + 1])
        WTs = sb("WTs", [P, D])
        asb = sb("asb", [P, 2])
        wa2 = sb("wa2", [P, P])
        ident = sb("ident", [P, P])
        identb = sb("identb", [P, P], bf16)
        future = sb("future", [P, P], bf16)
        iota16 = sb("iota16", [P, TOP])
        hoff = sb("hoff", [P, H])
        stat6 = sb("stat6", [P, NT, 6])
        mv = sb("mv", [P, NT, 2])
        sd = sb("sd", [P, NT])
        rstd = sb("rstd", [P, NT])
        epsc = sb("epsc", [P, 1])
        hn = sb("hn", [P, 2, 2, D])
        hTs = sb("hTs", [P, 2, 2 * P])
        gmax = sb("gmax", [P, 2])
        gneg = sb("gneg", [P, 2])
        gsum = sb("gsum", [P, 2])
        grec = sb("grec", [P, 2])
        prT = sb("prT", [P, 2, CH])
        sims = sb("sims", [P, 2, PS, NK])
        simr = sb("simr", [P, PS, NK])
        top = sb("top", [P, PS, TOP])
        topi = sb("topi", [P, PS, TOP], u32)
        HALF = TOP // 2
        BEHIND = HALF * TOP - HALF
        cand = sb("cand", [P, HALF, TOP])
        candr = sb("candr", [P, HALF * TOP])
        fin = sb("fin", [P, 2, TOP])
        finp = sb("finp", [P, TOP], u32)
        finr = sb("finr", [P, PS, TOP], u32)
        hot = sb("hot", [P, PS, TOP, TOP])
        part = sb("part", [P, PS, TOP])
        rowf = sb("rowf", [P, TOP])
        rowi = sb("rowi", [P, 2, TOP], u32)
        fneg = sb("fneg", [P, 2])
        fexp = sb("fexp", [P, 2, TOP])
        fsum = sb("fsum", [P, 2])
        frec = sb("frec", [P, 2])
        wmix = sb("wmix", [P, 2, TOP])
        qT = sb("qT", [P, P])
        rneg = sb("rneg", [P, 2])
        rsum = sb("rsum", [P, 2])
        rrec = sb("rrec", [P, 2])
        oS = sb("oS", [P, D])
        oT = sb("oT", [P, P])

        adjs = gath[:, :, :, :].rearrange("p b k d -> p b (k d)").bitcast(i32)
        mneg = gath[:, :, :, :].rearrange("p b k d -> p b (k d)")
        grow = [val[:, :, :].rearrange("p t d -> p (t d)"), srow[:, :]]
        hp = keyT[:, :].rearrange("p (t d) -> p t d", d=D)
        wh2b = xT
        elus = [wh2a[:, 0:FIRST * P], wh2a[:, FIRST * P:NP]]

        psS = [bank("psS0"), bank("psS1")]
        psT = [bank("psT0"), bank("psT1")]
        psO = bank("psO")
        psQ = bank("psQ")
        psY = bank("psY")
        psM = bank("psM")
        psG = [psO, psQ]
        ps_q, ps_k = psQ[:, 0:P], psQ[:, P:2 * P]
        ps_ot, ps_y = psY[:, 0:P], psY[:, P:2 * P]

        s_dve = sem("dve_step")
        x_loaded = sem("x_loaded")
        x_padded = sem("x_padded")
        w_loaded = sem("w_loaded")
        pk_loaded = sem("pk_loaded")
        wqo_loaded = sem("wqo_loaded")
        pool_step = sem("pool_step")
        consts_ready = sem("consts_ready")
        wa_ps, wa_ready = sem("wa_ps"), sem("wa_ready")
        simw_ps, simw_ready = sem("simw_ps"), sem("simw_ready")
        var_ready, sd_ready = sem("var_ready"), sem("sd_ready")
        norm_ready, normT_ps, normT_ready = sem("norm_ready"), sem("normT_ps"), sem("normT_ready")
        wh_ps, wh_ready, wh2_ready = sem("wh_ps"), sem("wh_ready"), sem("wh2_ready")
        var2_ready, sd2_ready = sem("var2_ready"), sem("sd2_ready")
        norm2_ready, norm2T_ps, norm2T_ready = sem("norm2_ready"), sem("norm2T_ps"), sem("norm2T_ready")
        adj_loaded = [sem("adj_loaded0"), sem("adj_loaded1")]
        gneg_ready, gexp_ready = sem("gneg_ready"), sem("gexp_ready")
        g_tps, g_pT, g_pv, g_out = sem("g_tps"), sem("g_pT"), sem("g_pv"), sem("g_out")
        elu_in, elu_exp = sem("elu_in"), sem("elu_exp")
        sims_ps, sims_ready, top_done = sem("sims_ps"), sem("sims_ready"), sem("top_done")
        fin_ready, fexp_ready, rows_ready = sem("fin_ready"), sem("fexp_ready"), sem("rows_ready")
        gathered = [[sem(f"gathered{q}_{g}") for g in range(TOP // GROUP)] for q in range(2)]
        kv_ready, k_ps, k_ready, v_ready = sem("kv_ready"), sem("k_ps"), sem("k_ready"), sem("v_ready")
        wq_ready, q_ps, q_ready = sem("wq_ready"), sem("q_ps"), sem("q_ready")
        s_ps, s_ready, rneg_ready, p_ready = sem("s_ps"), sem("s_ready"), sem("rneg_ready"), sem("p_ready")
        t_ps, pT_ready, pv_done = sem("t_ps"), sem("pT_ready"), sem("pv_done")
        rrec_ready = sem("rrec_ready")
        o_ready, ot_ps, ot_ready, y_ps, y_added = (
            sem("o_ready"), sem("ot_ps"), sem("ot_ready"), sem("y_ps"), sem("y_added"))
        stored = sem("stored")
        tick = {e: sem(f"tick_{e}") for e in ("pool", "dve", "act")}

        block = ctx.enter_context(nc.Block())

        def held(eng, name):
            eng.sem_inc(tick[name], 1)

        def pairs(eng, body, start):
            if (NT // 2 - start) % 2:
                body(start, start % 2)
                start += 1
            with eng.Fori(0, (NT // 2 - start) // 2) as r:
                for k in range(2):
                    body(r * 2 + (start + k), (start + k) % 2)

        def graph_tiles(eng, body):
            body(0, 0, 0)
            body(1, 1, 1)
            with eng.Fori(1, NT // 2) as r:
                for q in range(2):
                    body(r * 2 + q, q, 2)

        def every_head(eng, body):
            body(0, True, False)
            with eng.Fori(1, H - 1) as h:
                body(h, False, False)
            body(H - 1, False, True)

        def steps_of(first, last):
            for t in range(NT + 3 if last else NT):
                yield t, lambda d, t=t: not (first and t + d < 0) and not (last and t + d >= NT)

        def chunk0(t):
            return chunk_at[t % NT] + (t // NT) * NCH

        @block.sync
        def _(sp):
            full = NT - 1
            sp.dma_start(xs[:, 0:full, :], x[0:full * P, :].rearrange("(t p) d -> p t d", p=P)).then_inc(x_loaded, 16)
            sp.wait_ge(x_padded, 1)
            sp.dma_start(xs[0:SPLIT, full, :], x[full * P:full * P + SPLIT, :]).then_inc(x_loaded, 16)
            sp.dma_start(xs[SPLIT:REST, full, :], x[full * P + SPLIT:N, :]).then_inc(x_loaded, 16)
            sp.dma_start(Wsb[:, 0:D], W).then_inc(w_loaded, 16)
            sp.dma_start(WTs[:, :], WT).then_inc(w_loaded, 16)
            sp.dma_start(asb[:, :], a).then_inc(w_loaded, 16)

            def load_adj(i, q, rows):
                sp.dma_start(adjs[0:SPLIT, q, 0:N], adj[bass.ds(i * P, SPLIT), :]).then_inc(adj_loaded[q], 16)
                sp.dma_start(adjs[SPLIT:rows, q, 0:N], adj[bass.ds(i * P + SPLIT, rows - SPLIT), :])\
                    .then_inc(adj_loaded[q], 16)

            sp.dma_start(wpk[:, :, :], wqpkT.rearrange("s h k c -> k (s h) c")).then_inc(pk_loaded, 16)
            sp.dma_start(kpk[:, :, :], keysT.rearrange("s h k n -> k (s h) n")).then_inc(pk_loaded, 16)
            load_adj(0, 0, P)
            load_adj(1, 1, P)
            sp.dma_start(Wqs[:, :, :], Wq.rearrange("c (h d) -> c h d", h=H)).then_inc(wqo_loaded, 16)
            sp.dma_start(Wos[:, :, :], Wo.rearrange("(h d) n -> d h n", h=H)).then_inc(wqo_loaded, 16)
            with sp.Fori(1, NT // 2 - 1) as r:
                for q in range(2):
                    sp.wait_ge(gneg_ready, r * 2 + (q + 1))
                    load_adj(r * 2 + q, q, P)
            sp.wait_ge(gneg_ready, NT - 1)
            load_adj(NT - 2, 0, P)
            sp.wait_ge(gneg_ready, NT)
            load_adj(NT - 1, 1, REST)
            for t in range(NT):
                rows = P if t < full else REST
                sp.wait_ge(y_added, (H - 1) * NT + t + 1)
                if rows == P:
                    sp.dma_start(out[t * P:t * P + rows, :], xs[:, t, :]).then_inc(stored, 16)
                else:
                    sp.dma_start(out[t * P:t * P + SPLIT, :], xs[0:SPLIT, t, :]).then_inc(stored, 16)
                    sp.dma_start(out[t * P + SPLIT:N, :], xs[SPLIT:rows, t, :]).then_inc(stored, 16)
            sp.wait_ge(stored, 16 * (NT + (REST < P)))

        @block.gpsimd
        def _(pool):
            nc.gpsimd.memset(ident[:, :], 0.0).then_inc(pool_step, 1)
            nc.gpsimd.memset(future[:, :], 0.0).then_inc(pool_step, 1)
            nc.gpsimd.memset(epsc[:, :], EPS)
            nc.gpsimd.memset(prow[:, :, N:NP], 0.0)
            nc.gpsimd.iota(iota16[:, :], [[1, TOP]], base=0, channel_multiplier=0,
                           allow_small_or_imprecise_dtypes=True)
            nc.gpsimd.iota(hoff[:, :], [[NK * NK, H]], base=0, channel_multiplier=0,
                           allow_small_or_imprecise_dtypes=True)
            pool.wait_ge(pool_step, 2)
            nc.gpsimd.affine_select(out=ident[:, :], in_=ident[:, :], compare_op=ALU.not_equal, fill=1.0,
                                    base=0, pattern=[[-1, P]], channel_multiplier=1).then_inc(pool_step, 1)
            nc.gpsimd.affine_select(out=future[:, :], in_=future[:, :], compare_op=ALU.is_ge, fill=FUTURE,
                                    base=0, pattern=[[-1, P]], channel_multiplier=1).then_inc(pool_step, 1)
            pool.wait_ge(pool_step, 4)
            nc.gpsimd.tensor_copy(identb[:, :], ident[:, :]).then_inc(consts_ready, 1)

            def head(h, first, last):
                for t in range(NT):
                    q = t % 2
                    pool.wait_ge(rows_ready, h * NT + (t + 1))
                    pool.wait_ge(kv_ready, h * NT + (t + 1))
                    held(pool, "pool")
                    for k in range(TOP):
                        pool.indirect_dma_start(gath[:, q, k, :], None, kv_table,
                                                bass.IndirectOffsetOnAxis(ap=rowi[:, q, k:k + 1], axis=0))\
                            .then_inc(gathered[q][k // GROUP], 16)

            every_head(pool, head)

        @block.tensor
        def _(pe):
            mm, tr = nc.tensor.matmul, nc.tensor.transpose
            pe.wait_ge(w_loaded, 48)
            mm(psM[:, 0:2], WTs[:, :], asb[:, :], start=True, stop=True).then_inc(wa_ps, 1)
            pe.wait_ge(consts_ready, 1)
            pe.wait_ge(wa_ready, 1)

            pe.wait_ge(pk_loaded, 32)
            for h in range(H):
                if h >= 2:
                    pe.wait_ge(simw_ready, h - 1)
                for s in range(PS):
                    last = mm(psT[h % 2][:, s * NK:(s + 1) * NK], wpk[:, s * H + h, :], kpk[:, s * H + h, :],
                              start=True, stop=True)
                last.then_inc(simw_ps, 1)
            pe.wait_ge(simw_ready, H)

            def turn_pair(u, b):
                pe.wait_ge(norm_ready, u + 1)
                pe.wait_ge(normT_ready, u + 1)
                tr(psT[b][:, 0:P], hn[:, b, 0, :], ident[:, :])
                tr(psT[b][:, P:2 * P], hn[:, b, 1, :], ident[:, :]).then_inc(normT_ps, 1)

            def wh_pair(u, b):
                pe.wait_ge(normT_ready, u + 3)
                pe.wait_ge(wh_ready, u + 1)
                pe.wait_ge(wh2_ready, u + 1)
                for q in range(2):
                    mm(psS[b][:, q * (D + 1):(q + 1) * (D + 1)], hTs[:, b, q * P:(q + 1) * P], Wsb[:, :],
                       start=True, stop=True)
                mm(psG[b][:, 0:2 * P], wa2[:, :], hTs[:, b, :], start=True, stop=True).then_inc(wh_ps, 1)

            def norm_pair(u, b):
                turn_pair(u, b)
                wh_pair(u - 1, 1 - b)

            turn_pair(0, 0)
            pairs(pe, norm_pair, 1)
            wh_pair(NT // 2 - 1, (NT // 2 - 1) % 2)
            pe.wait_ge(wh_ready, NT // 2 + 2)
            pe.wait_ge(wh2_ready, NT // 2 + 2)

            def graph_row(i, q):
                pe.wait_ge(gexp_ready, i + 3)
                pe.wait_ge(g_out, i + 1)

                def turn(c):
                    pe.wait_ge(g_pT, i * GC + (c + 1))
                    for b in range(min(C, NT - C * c)):
                        last = tr(psT[turned[0] % 2][:, b * P:(b + 1) * P],
                                  prow[:, q, (C * c + b) * P:(C * c + b + 1) * P], ident[:, :])
                    last.then_inc(g_tps, 1)
                    turned[0] += 1

                turned = [(q * GC) % 2]
                turn(0)
                for c in range(GC):
                    if c + 1 < GC:
                        turn(c + 1)
                    pe.wait_ge(g_pT, i * GC + (c + 3))
                    for b in range(min(C, NT - C * c)):
                        j = C * c + b
                        last = mm(psG[q][:, 0:D], prT[:, (q * GC + c) % 2, b * P:(b + 1) * P], Whx[:, j, 0:D],
                                  start=(j == 0), stop=(j == NT - 1))
                    last.then_inc(g_pv, 1)

            with pe.Fori(0, NT // 2 - 1) as r:
                for q in range(2):
                    graph_row(r * 2 + q, q)
            graph_row(NT - 2, 0)

            def norm2_pair(u, b):
                pe.wait_ge(norm2_ready, u + 1)
                pe.wait_ge(norm2T_ready, u + 1)
                tr(psS[b][:, 0:P], hn[:, b, 0, :], ident[:, :])
                tr(psS[b][:, P:2 * P], hn[:, b, 1, :], ident[:, :]).then_inc(norm2T_ps, 1)

            norm2_pair(0, 0)
            norm2_pair(1, 1)
            pe.wait_ge(norm2T_ready, 4)

            def find_sims(h, t):
                mm(psM[:, 0:PS * NK], xT[:, t * P:(t + 1) * P],
                   simw[:, bass.ds(h, 1), :, :].rearrange("p o s k -> p (o s k)"), start=True, stop=True)\
                    .then_inc(sims_ps, 1)

            find_sims(0, 0)
            pe.wait_ge(sims_ready, 1)
            find_sims(0, 1)
            graph_row(NT - 1, 1)
            pe.wait_ge(sims_ready, 2)
            find_sims(0, 2)
            pairs(pe, norm2_pair, FIRST // 2)
            pe.wait_ge(norm2T_ready, NT // 2 + 2)

            def head(h, first, last):
                def project(t):
                    pe.wait_ge(ot_ready, h * NT + (t + 1))
                    mm(ps_y, oT[:, :], Wos[:, bass.ds(h + t // NT, 1), :].rearrange("p o d -> p (o d)"),
                       start=True, stop=True).then_inc(y_ps, 1)

                def turn(t, c):
                    g = chunk0(t) + c
                    pe.wait_ge(pT_ready, h * NCH + (g + 1))
                    for b in range(min(C, t % NT + 1 - c * C)):
                        one = tr(psT[g % 2][:, b * P:(b + 1) * P],
                                 prow[:, t % 2, (c * C + b) * P:(c * C + b + 1) * P], ident[:, :])
                    one.then_inc(t_ps, 1)

                def attend(t):
                    pe.wait_ge(p_ready, h * NT + (t + 1))
                    pe.wait_ge(v_ready, h * NT + (t + 3))
                    n = chunks_of[t % NT]
                    turn(t, 0)
                    for c in range(n):
                        g = chunk0(t) + c
                        if c + 1 < n:
                            turn(t, c + 1)
                        pe.wait_ge(pT_ready, h * NCH + (g + 3))
                        for b in range(min(C, t % NT + 1 - c * C)):
                            j = c * C + b
                            one = mm(psO[:, 0:D], prT[:, g % 2, b * P:(b + 1) * P], val[:, j, :],
                                     start=(j == 0), stop=(j == t % NT))
                        one.then_inc(pv_done, 1)

                def score(t):
                    pe.wait_ge(q_ready, h * NT + (t + 1))
                    pe.wait_ge(kv_ready, h * NT + (t + 3))
                    tr(ps_k, kvm[:, t % 2, 0:D], ident[:, :]).then_inc(k_ps, 1)
                    pe.wait_ge(k_ready, h * NT + (t + 1))
                    for c in range(chunks_of[t]):
                        g = chunk0(t) + c
                        w = min(CH, (t + 1) * P - c * CH)
                        pe.wait_ge(s_ready, h * NCH + (g + 1))
                        diagonal = c == chunks_of[t] - 1
                        one = mm(psS[g % 2][:, 0:w], qT[:, :], keyT[:, c * CH:c * CH + w],
                                 start=True, stop=not diagonal)
                        if diagonal:
                            one = mm(psS[g % 2][:, w - P:w], identb[:, :], future[:, :], start=False, stop=True)
                        one.then_inc(s_ps, 1)

                for t, there in steps_of(first, last):
                    if there(-3):
                        project(t - 3)
                    if there(3):
                        pe.wait_ge(sims_ready, h * NT + (t + 3))
                        find_sims(h + (t + 3) // NT, (t + 3) % NT)
                    if there(0):
                        if t == 0:
                            pe.wait_ge(wq_ready, h + 1)
                        mm(ps_q, wq_now[:, :], xT[:, t * P:(t + 1) * P], start=True, stop=True).then_inc(q_ps, 1)
                    if there(-2):
                        attend(t - 2)
                    if there(0):
                        score(t)
                    if there(-2):
                        pe.wait_ge(o_ready, h * NT + (t - 1))
                        if there(-3):
                            pe.wait_ge(y_added, h * NT + (t - 2))
                        tr(ps_ot, oS[:, :], ident[:, :]).then_inc(ot_ps, 1)

            every_head(pe, head)

        @block.scalar
        def _(act):
            def copy(dst, src):
                return nc.scalar.activation(dst, src, ACT.Copy)

            for room in (normT_ready, wh2_ready, norm2T_ready, gexp_ready, s_ready, g_pT, pT_ready, v_ready):
                act.sem_inc(room, 2)
            for h in range(H):
                act.wait_ge(simw_ps, h + 1)
                copy(simw[:, h, :, :], psT[h % 2][:, 0:PS * NK].rearrange("p (s k) -> p s k", s=PS))\
                    .then_inc(simw_ready, 1)
            act.wait_ge(var_ready, 1)
            act.wait_ge(consts_ready, 1)
            nc.scalar.activation(sd[:, :], mv[:, :, 1], ACT.Sqrt, bias=epsc[:, 0:1]).then_inc(sd_ready, 1)

            def turn_pair(u, b):
                act.wait_ge(normT_ps, u + 1)
                copy(hTs[:, b, :], psT[b][:, 0:2 * P]).then_inc(normT_ready, 1)

            def wh2_pair(u, b):
                act.wait_ge(wh_ps, u + 1)
                held(act, "act")
                nc.scalar.activation(wh2a[:, bass.ds(u * (2 * P), 2 * P)], psG[b][:, 0:2 * P], ACT.Copy, scale=ALPHA)
                nc.scalar.activation(wh2b[:, bass.ds(u * (2 * P), 2 * P)], psG[b][:, 0:2 * P], ACT.Copy,
                                     scale=1.0 - ALPHA).then_inc(wh2_ready, 1)

            def norm_pair(u, b):
                turn_pair(u, b)
                wh2_pair(u - 1, 1 - b)

            turn_pair(0, 0)
            pairs(act, norm_pair, 1)
            wh2_pair(NT // 2 - 1, (NT // 2 - 1) % 2)

            def graph_chunks(i, q, some):
                for c in some:
                    act.wait_ge(g_pv, i * GC + (c + 1))
                    act.wait_ge(g_tps, i * GC + (c + 1))
                    w = min(C, NT - C * c) * P
                    copy(prT[:, (q * GC + c) % 2, 0:w], psT[(q * GC + c) % 2][:, 0:w]).then_inc(g_pT, 1)

            def graph_tile(i, q, before):
                if before >= 1:
                    graph_chunks(i - 1, 1 - q, range(GC // 2 + 1))
                act.wait_ge(gneg_ready, i + 3)
                nc.scalar.activation(prow[:, q, 0:N], grow[q][:, 0:N], ACT.Exp, bias=gneg[:, q:q + 1],
                                     accum_out=gsum[:, q:q + 1]).then_inc(gexp_ready, 1)
                if before >= 1:
                    graph_chunks(i - 1, 1 - q, range(GC // 2 + 1, GC))

            graph_tiles(act, graph_tile)

            def elu_and_deviation(n, tiles):
                act.wait_ge(elu_in, n + 1)
                nc.scalar.activation(elus[n], elus[n], ACT.Exp).then_inc(elu_exp, 1)
                act.wait_ge(var2_ready, n + 1)
                nc.scalar.activation(sd[:, tiles], mv[:, tiles, 1], ACT.Sqrt, bias=epsc[:, 0:1])\
                    .then_inc(sd2_ready, 1)

            elu_and_deviation(0, slice(0, FIRST))

            def norm2_pair(u, b):
                act.wait_ge(norm2T_ps, u + 1)
                held(act, "act")
                copy(xT[:, bass.ds(u * (2 * P), 2 * P)], psS[b][:, 0:2 * P]).then_inc(norm2T_ready, 1)

            norm2_pair(0, 0)
            norm2_pair(1, 1)

            def sims_out(n, q):
                act.wait_ge(sims_ps, n + 1)
                copy(sims[:, q, :, :], psM[:, 0:PS * NK].rearrange("p (s k) -> p s k", s=PS))\
                    .then_inc(sims_ready, 1)

            def weights(n, q):
                act.wait_ge(fin_ready, n + 1)
                nc.scalar.activation(fexp[:, q, :], fin[:, q, :], ACT.Exp, bias=fneg[:, q:q + 1],
                                     accum_out=fsum[:, q:q + 1]).then_inc(fexp_ready, 1)

            sims_out(0, 0)
            sims_out(1, 1)
            graph_chunks(NT - 1, 1, range(GC))
            weights(0, 0)
            weights(1, 1)
            elu_and_deviation(1, slice(FIRST, NT))
            act.wait_ge(top_done, 1)
            sims_out(2, 0)
            pairs(act, norm2_pair, FIRST // 2)
            act.wait_ge(wqo_loaded, 32)

            def head(h, first, last):
                if not (first or last):
                    held(act, "act")
                copy(wq_now[:, :], Wqs[:, bass.ds(h, 1), :].rearrange("p o d -> p (o d)")).then_inc(wq_ready, 1)
                for t, there in steps_of(first, last):
                    q = t % 2

                    def values():
                        copy(val[:, (t - 1) % NT, :], kvm[:, 1 - q, D:KV]).then_inc(v_ready, 1)

                    if there(-1) and t != 1:
                        values()
                    if there(3):
                        act.wait_ge(top_done, h * NT + (t + 2))
                        sims_out(h * NT + (t + 3), 1 - q)
                    if there(0):
                        act.wait_ge(q_ps, h * NT + (t + 1))
                        nc.scalar.activation(qT[:, :], ps_q, ACT.Copy, scale=SCALE).then_inc(q_ready, 1)
                    if there(2):
                        weights(h * NT + (t + 2), q)

                    def exponentials():
                        w = ((t - 1) % NT + 1) * P
                        act.wait_ge(rneg_ready, h * NT + t)
                        nc.scalar.activation(prow[:, 1 - q, 0:w], srow[:, 0:w], ACT.Exp,
                                             bias=rneg[:, 1 - q:2 - q], accum_out=rsum[:, 1 - q:2 - q])\
                            .then_inc(p_ready, 1)

                    early = there(-2) and there(-1) and chunks_of[(t - 2) % NT] >= LONG
                    if there(-2):
                        for c in range(chunks_of[(t - 2) % NT]):
                            g = chunk0(t - 2) + c
                            w = min(CH, ((t - 2) % NT + 1) * P - c * CH)
                            act.wait_ge(pv_done, h * NCH + (g + 1))
                            act.wait_ge(t_ps, h * NCH + (g + 1))
                            copy(prT[:, g % 2, 0:w], psT[g % 2][:, 0:w]).then_inc(pT_ready, 1)
                            if early and c == LONG - 1:
                                exponentials()
                        act.wait_ge(rrec_ready, h * NT + (t - 1))
                        act.wait_ge(pv_done, h * NCH + (chunk0(t - 1) + 2))
                        nc.scalar.activation(oS[:, :], psO[:, 0:D], ACT.Copy, scale=rrec[:, q:q + 1])\
                            .then_inc(o_ready, 1)
                    if t == 1:
                        values()
                    if there(-1) and not early:
                        exponentials()
                    if there(0):
                        act.wait_ge(k_ps, h * NT + (t + 1))
                        copy(keyT[:, t * P:(t + 1) * P], ps_k).then_inc(k_ready, 1)
                        for c in range(chunks_of[t]):
                            g = chunk0(t) + c
                            w = min(CH, (t + 1) * P - c * CH)
                            act.wait_ge(s_ps, h * NCH + (g + 1))
                            copy(srow[:, c * CH:c * CH + w], psS[g % 2][:, 0:w]).then_inc(s_ready, 1)
                    if there(-2):
                        act.wait_ge(ot_ps, h * NT + (t - 1))
                        copy(oT[:, :], ps_ot).then_inc(ot_ready, 1)

            every_head(act, head)

        @block.vector
        def _(dve):
            v = nc.vector
            steps = [0]

            def step(ins):
                steps[0] += 1
                ins.then_inc(s_dve, 1)
                return steps[0]

            def need(k):
                dve.wait_ge(s_dve, k)

            def restart():
                dve.wait_ge(s_dve, steps[0])
                dve.sem_clear(s_dve)
                steps[0] = 0

            for room in (wh_ready, gneg_ready, g_out, g_pv, kv_ready, pv_done):
                dve.sem_inc(room, 2)
            v.memset(xs[:, NT - 1, :], 0.0).then_inc(x_padded, 1)
            dve.wait_ge(wa_ps, 1)
            v.tensor_scalar(Wsb[:, D:D + 1], psM[:, 0:1], ALPHA - 1.0, None, ALU.mult)
            v.tensor_copy(wa2[:, :], psM[:, 1:2].to_broadcast([P, P])).then_inc(wa_ready, 1)
            dve.wait_ge(x_loaded, 48)

            def stats(tiles, done):
                filled = {t: step(v.bn_stats(stat6[:, t, :], xs[:, t, :])) for t in tiles}
                for t in tiles:
                    need(filled[t])
                    one = v.bn_aggr(mv[:, t, :], stat6[:, t, :])
                one.then_inc(done, 1)

            def normalize(u, b):
                for q in range(2):
                    i = u * 2 + q
                    one = v.tensor_scalar(hn[:, b, q, :], xs[:, bass.ds(i, 1), :].rearrange("p o d -> p (o d)"),
                                          mv[:, bass.ds(i, 1), 0:1].rearrange("p o d -> p (o d)"),
                                          rstd[:, bass.ds(i, 1)], ALU.subtract, ALU.mult)
                return one

            stats(range(NT), var_ready)
            dve.wait_ge(sd_ready, 1)
            k = step(v.reciprocal(rstd[:, :], sd[:, :]))
            need(k)
            restart()

            def wh_out(u, b):
                dve.wait_ge(wh_ps, u + 1)
                held(dve, "dve")
                v.tensor_copy(Whx[:, bass.ds(u * 2, 2), :].rearrange("p o d -> p (o d)"), psS[b][:, 0:2 * (D + 1)])\
                    .then_inc(wh_ready, 1)

            def norm_pair(u, b):
                dve.wait_ge(normT_ready, u + 1)
                normalize(u, b).then_inc(norm_ready, 1)
                wh_out(u - 1, 1 - b)

            normalize(0, 0).then_inc(norm_ready, 1)
            pairs(dve, norm_pair, 1)
            wh_out(NT // 2 - 1, (NT // 2 - 1) % 2)

            dve.wait_ge(wh2_ready, NT // 2 + 2)

            def graph_denominator(i, q):
                dve.wait_ge(gexp_ready, i + 3)
                step(v.reciprocal(grec[:, q:q + 1], gsum[:, q:q + 1]))

            def graph_out(i, q):
                need(steps[0])
                dve.wait_ge(g_pv, i * GC + (GC + 2))
                v.tensor_scalar(hp[:, bass.ds(i, 1), :].rearrange("p o d -> p (o d)"), psG[q][:, 0:D],
                                grec[:, q:q + 1], None, ALU.mult).then_inc(g_out, 1)

            def graph_tile(i, q, before):
                steps[0] = 0
                dve.wait_ge(adj_loaded[q], (i + (2 - q)) * 16)
                step(v.tensor_scalar(mneg[:, q, 0:N], adjs[:, q, 0:N], 0.0, MASKED, ALU.is_le, ALU.mult))
                if before >= 2:
                    graph_denominator(i - 2, q)
                dve.wait_ge(gexp_ready, i + 1)
                held(dve, "dve")
                m = step(v.scalar_tensor_tensor(grow[q][:, 0:N], wh2b[:, 0:N],
                                                Whx[:, bass.ds(i, 1), D:D + 1].rearrange("p o d -> p (o d)"),
                                                wh2a[:, 0:N], ALU.max, ALU.add))
                need(m)
                m = step(v.tensor_tensor_reduce(out=grow[q][:, 0:N], in0=grow[q][:, 0:N], in1=mneg[:, q, 0:N],
                                                scale=1.0, scalar=LOWEST, op0=ALU.add, op1=ALU.max,
                                                accum_out=gmax[:, q:q + 1]))
                need(m)
                v.tensor_scalar(gneg[:, q:q + 1], gmax[:, q:q + 1], -1.0, None, ALU.mult).then_inc(gneg_ready, 1)
                if before >= 2:
                    graph_out(i - 2, q)
                restart()

            graph_tiles(dve, graph_tile)

            def elu_and_norm(n, tiles):
                h_flat = hp[:, tiles, :].rearrange("p t d -> p (t d)")
                x_flat = xs[:, tiles, :].rearrange("p t d -> p (t d)")
                v.tensor_scalar(elus[n], h_flat, 0.0, None, ALU.min).then_inc(elu_in, 1)
                k = step(v.scalar_tensor_tensor(x_flat, h_flat, 0.0, x_flat, ALU.max, ALU.add))
                need(k)
                dve.wait_ge(elu_exp, n + 1)
                k = step(v.scalar_tensor_tensor(x_flat, elus[n], -1.0, x_flat, ALU.add, ALU.add))
                need(k)
                stats(range(NT)[tiles], var2_ready)
                dve.wait_ge(sd2_ready, n + 1)
                k = step(v.reciprocal(rstd[:, tiles], sd[:, tiles]))
                need(k)
                restart()

            def norm2_pair(u, b):
                dve.wait_ge(norm2T_ready, u + 1)
                normalize(u, b).then_inc(norm2_ready, 1)

            dve.wait_ge(g_out, FIRST + 2)
            elu_and_norm(0, slice(0, FIRST))
            norm2_pair(0, 0)
            norm2_pair(1, 1)

            def search(h, n, q, mix, largest):
                dve.wait_ge(sims_ready, n + 1)
                held(dve, "dve")
                part1 = [step(v.max(top[:, s, 0:8], sims[:, q, s, :])) for s in range(PS)]
                mix(5)
                need(part1[1])
                for s in range(PS):
                    cut = step(v.match_replace(simr[:, s, :], top[:, s, 0:8], sims[:, q, s, :], LOWEST))
                for s in range(PS):
                    i1 = step(v.max_index(topi[:, s, 0:8], top[:, s, 0:8], sims[:, q, s, :]))
                need(cut)
                part2 = [step(v.max(top[:, s, 8:16], simr[:, s, :])) for s in range(PS)]
                mix(6)
                need(i1)
                dve.sem_inc(top_done, 1)
                need(part2[1])
                flat = cand[:, :, :].rearrange("p a b -> p (a b)")
                sums = step(v.tensor_tensor(cand[:, :, :],
                                            top[:, 0, 0:HALF].unsqueeze(2).to_broadcast([P, HALF, TOP]),
                                            top[:, 1, :].unsqueeze(1).to_broadcast([P, HALF, TOP]), ALU.add))
                v.max_index(topi[:, 0, 8:16], top[:, 0, 8:16], simr[:, 0, :])
                need(sums)
                sums = step(v.tensor_scalar(cand[:, HALF - 1, TOP - HALF:TOP], top[:, 0, HALF:TOP],
                                            top[:, 1, 0:1], None, ALU.add))
                i2 = step(v.max_index(topi[:, 1, 8:16], top[:, 1, 8:16], simr[:, 1, :]))
                need(sums)
                f1 = step(v.max(fin[:, q, 0:8], flat))
                mix(7)
                need(f1)
                cut = step(v.match_replace(candr[:, :], fin[:, q, 0:8], flat, LOWEST))
                v.max_index(finp[:, 0:8], fin[:, q, 0:8], flat)
                need(cut)
                f2 = step(v.max(fin[:, q, 8:16], candr[:, :]))
                mix(8)
                v.tensor_scalar(fneg[:, q:q + 1], fin[:, q, 0:1], -1.0, None, ALU.mult).then_inc(fin_ready, 1)
                need(f2)
                p2 = step(v.max_index(finp[:, 8:16], fin[:, q, 8:16], candr[:, :]))
                mix(9)
                need(p2)
                v.tensor_scalar(finr[:, 0, :], finp[:, :], 4, None, ALU.logical_shift_right)
                ranks = step(v.tensor_scalar(finr[:, 1, :], finp[:, :], TOP - 1, None, ALU.bitwise_and))
                mix(10)
                need(ranks)
                v.scalar_tensor_tensor(finr[:, 0, :], finp[:, :], float(BEHIND - HALF), finr[:, 0, :],
                                       ALU.subtract, ALU.max)
                ranks = step(v.scalar_tensor_tensor(finr[:, 1, :], finp[:, :], float(BEHIND), finr[:, 1, :],
                                                    ALU.is_lt, ALU.mult))
                largest()
                mix(11)
                need(ranks)
                both = [P, PS, TOP, TOP]
                hot1 = step(v.tensor_tensor(hot[:, :, :, :], finr[:, :, :].unsqueeze(3).to_broadcast(both),
                                            iota16[:, :].unsqueeze(1).unsqueeze(1).to_broadcast(both),
                                            ALU.is_equal))
                mix(12)
                need(hot1)
                need(i2)
                hot2 = step(v.tensor_tensor(hot[:, :, :, :], hot[:, :, :, :],
                                            topi[:, :, :].unsqueeze(2).to_broadcast(both), ALU.mult))
                mix(13)
                need(hot2)
                keys = step(v.tensor_reduce(part[:, :, :].rearrange("p s k -> p (s k)"),
                                            hot[:, :, :, :].rearrange("p s k r -> p (s k) r"), AX.X, ALU.add))
                mix(14)
                need(keys)
                rows = step(v.scalar_tensor_tensor(rowf[:, :], part[:, 1, :], float(NK), part[:, 0, :],
                                                   ALU.mult, ALU.add))
                mix(15)
                need(rows)
                v.tensor_scalar(rowi[:, q, :], rowf[:, :], hoff[:, bass.ds(h, 1)], None, ALU.add)\
                    .then_inc(rows_ready, 1)

            def weigh1(n, q):
                dve.wait_ge(fexp_ready, n + 1)
                return step(v.reciprocal(frec[:, q:q + 1], fsum[:, q:q + 1]))

            def weigh2(r, q):
                need(r)
                return step(v.tensor_scalar(wmix[:, q, :], fexp[:, q, :], frec[:, q:q + 1], None, ALU.mult))

            def nothing(*_):
                pass

            search(0, 0, 0, nothing, nothing)
            search(0, 1, 1, nothing, nothing)
            restart()
            for q in range(2):
                graph_denominator(NT - 2 + q, q)
                graph_out(NT - 2 + q, q)
            dve.wait_ge(g_out, NT + 2)
            elu_and_norm(1, slice(FIRST, NT))
            pairs(dve, norm2_pair, FIRST // 2)
            weigh2(weigh1(0, 0), 0)
            restart()

            def head(h, first, last):
                steps[0] = 0
                for t, there in steps_of(first, last):
                    q = t % 2
                    done = [0]

                    def mix(k):
                        if not there(0):
                            return
                        dst = kvm[:, q, :]
                        if k % GROUP == 0:
                            dve.wait_ge(gathered[q][k // GROUP],
                                        h * (16 * GROUP * NT // 2) + 16 * GROUP * (t // 2 + 1))
                        if k == 0:
                            dve.wait_ge(v_ready, h * NT + (t + 1))
                            done[0] = step(v.tensor_scalar(dst, gath[:, q, 0, :], wmix[:, q, 0:1], None, ALU.mult))
                            return
                        need(done[0])
                        one = v.scalar_tensor_tensor(dst, gath[:, q, k, :], wmix[:, q, k:k + 1], dst,
                                                     ALU.mult, ALU.add)
                        if k < TOP - 1:
                            done[0] = step(one)
                        else:
                            one.then_inc(kv_ready, 1)

                    mix(0)
                    if there(1):
                        r = weigh1(h * NT + (t + 1), 1 - q)
                    mix(1)
                    if there(1):
                        weigh2(r, 1 - q)
                    mix(2)
                    mix(3)
                    mix(4)

                    def largest():
                        if there(-1):
                            dve.wait_ge(s_ready, h * NCH + (chunk0(t) + 2))
                            v.tensor_reduce(rneg[:, 1 - q:2 - q], srow[:, 0:((t - 1) % NT + 1) * P], AX.X,
                                            ALU.max, negate=True).then_inc(rneg_ready, 1)
                        if there(-3):
                            dve.wait_ge(y_ps, h * NT + (t - 2))
                            u = (t - 3) % NT
                            v.tensor_tensor(xs[:, u, :], xs[:, u, :], ps_y, ALU.add).then_inc(y_added, 1)
                        if there(-2):
                            dve.wait_ge(p_ready, h * NT + (t - 1))
                            v.reciprocal(rrec[:, q:q + 1], rsum[:, q:q + 1]).then_inc(rrec_ready, 1)

                    if there(2):
                        search(h + (t + 2) // NT, h * NT + (t + 2), q, mix, largest)
                    else:
                        for k in range(5, TOP):
                            mix(k)
                        largest()
                restart()

            every_head(dve, head)


def kernel(x, adj, L0_gnn_W, L0_gnn_a, L0_ffn_Wq_pk, L0_ffn_pk_keys, L0_ffn_Wq, L0_ffn_keys_table,
           L0_ffn_values_table, L0_ffn_Wo):
    import numpy as np
    import concourse.bacc as bacc
    from concourse import mybir
    from concourse.bass_utils import run_bass_kernel_spmd

    parts, keys, heads, width = L0_ffn_pk_keys.shape
    dim = x.shape[1]
    arrays = {
        "x": x,
        "adj": adj,
        "W": L0_gnn_W,
        "WT": np.asarray(L0_gnn_W).T,
        "a": np.asarray(L0_gnn_a).reshape(2, dim).T,
        "wqpkT": np.asarray(L0_ffn_Wq_pk).T.reshape(parts, heads, width, dim),
        "keysT": np.asarray(L0_ffn_pk_keys).transpose(0, 2, 3, 1),
        "Wq": L0_ffn_Wq,
        "kv_table": np.concatenate([np.asarray(L0_ffn_keys_table), np.asarray(L0_ffn_values_table)], axis=1),
        "Wo": L0_ffn_Wo,
    }
    nc = bacc.Bacc("TRN2", target_bir_lowering=False, num_devices=1)
    ins, args = {}, []
    for name, value in arrays.items():
        value = np.ascontiguousarray(value)
        ins[f"in_{name}"] = value
        args.append(nc.dram_tensor(f"in_{name}", value.shape, mybir.dt.from_np(value.dtype), kind="ExternalInput").ap())
    args.append(nc.dram_tensor("out_x", tuple(x.shape), mybir.dt.from_np(np.dtype("float32")), kind="ExternalOutput").ap())
    gat_then_product_key_attention(nc, *args)
    run = run_bass_kernel_spmd(nc, [ins], core_ids=[0])
    return run.results[0]["out_x"]
```
